# Optimizing a Trainium2 kernel written in Bass

```python
import numpy as np
import jax
import jax.numpy as jnp

def _softmax(x, axis=-1):
    return jax.nn.softmax(x, axis=axis)

def _gelu(x):
    return jax.nn.gelu(x, approximate=True)

def _silu(x):
    return jax.nn.silu(x)

def _sigmoid(x):
    return jax.nn.sigmoid(x)

def _layernorm(x, axis=-1, eps=1e-05):
    m = jnp.mean(x, axis=axis, keepdims=True)
    v = jnp.var(x, axis=axis, keepdims=True)
    return (x - m) / jnp.sqrt(v + eps)

def _scatter_add(tgt, idx, src, axis=0):
    return tgt.at[idx].add(src)

def _segment_sum(src, seg, n):
    return jax.ops.segment_sum(src, seg, n)
kernel_name = 'mk_decoder_postln_d1_seqx_r8_4ee709'

def setup_inputs(seed: int=0):
    np.random.seed(seed)
    _w = jnp.asarray

    def _rec_inputs():
        import jax
        import jax.numpy as jnp
        _rk = jax.random.key(seed)
        x = -0.0002928 + 1 * jax.random.normal(jax.random.fold_in(_rk, 1), (2, 256, 128), jnp.float32)
        _lenS = 256 - jax.random.randint(jax.random.fold_in(_rk, 7), (2,), 0, max(1, 256 // 4) + 1, jnp.int32)
        _lenS2 = 512 - jax.random.randint(jax.random.fold_in(_rk, 8), (2,), 0, max(1, 512 // 4) + 1, jnp.int32)
        _ctx_1024P = jax.random.normal(jax.random.fold_in(_rk, 11), (2, 16, 128), jnp.float32)
        _ctx_1024c = jax.random.dirichlet(jax.random.fold_in(_rk, 511), 0.3 * jnp.ones((16,), jnp.float32), (2, 512))
        _ctx_1024t = jnp.einsum('bsk,bkd->bsd', _ctx_1024c, _ctx_1024P)
        _ctx_1024t = _ctx_1024t * jax.lax.rsqrt(jnp.mean(jnp.square(_ctx_1024t)) + 1e-12) * 0.953939
        ctx_1024 = -1.39393e-06 + 0.999914 * (_ctx_1024t + 0.3 * jax.random.normal(jax.random.fold_in(_rk, 611), (2, 512, 128), jnp.float32))
        return (x, ctx_1024)
    x, ctx_1024 = _rec_inputs()

    def _L0_attn_setup():
        import jax, jax.numpy as jnp
        import numpy as np
        import math
        B, L, D = (8, 256, 128)
        HEADS = 1
        HIDDEN = 256
        INNER = HIDDEN // HEADS
        CAPACITY = 0.5
        ROUTER_K = math.ceil(L * CAPACITY)
        key = jax.random.key(seed)
        ks = jax.random.split(key, 6)
        s = 0.02
        return {'x': jax.random.normal(ks[0], (B, L, D), jnp.float32), 'router_w': jax.random.normal(ks[1], (1, D), jnp.float32) * s, 'router_b': jnp.zeros((1,), jnp.float32), 'wq': jax.random.normal(ks[2], (INNER, D), jnp.float32) * s, 'wk': jax.random.normal(ks[3], (INNER, D), jnp.float32) * s, 'wv': jax.random.normal(ks[4], (INNER, D), jnp.float32) * s}
    _L0_attn_all = _L0_attn_setup()
    _L0_attn_in = {k: v for k, v in _L0_attn_all.items() if k in ('router_w', 'router_b', 'wq', 'wk', 'wv')}
    del _L0_attn_all

    def _L0_xattn_setup():
        import jax, jax.numpy as jnp
        import numpy as np
        HIDDEN = 128
        NUM_HEADS = 16
        HEAD_DIM = HIDDEN // NUM_HEADS
        key = jax.random.key(seed)
        ks = jax.random.split(key, 10)
        B, T, S = (2, 256, 256)
        sc = 1.0 / np.sqrt(HIDDEN)
        inp = {'tgt': jax.random.normal(ks[0], (B, T, HIDDEN), jnp.float32), 'src': jax.random.normal(ks[1], (B, S, HIDDEN), jnp.float32), 'Wq': jax.random.normal(ks[2], (NUM_HEADS, HIDDEN, HEAD_DIM), jnp.float32) * sc, 'bq': jnp.zeros((NUM_HEADS, HEAD_DIM), jnp.float32), 'Wk': jax.random.normal(ks[3], (NUM_HEADS, HIDDEN, HEAD_DIM), jnp.float32) * sc, 'bk': jnp.zeros((NUM_HEADS, HEAD_DIM), jnp.float32), 'Wv': jax.random.normal(ks[4], (NUM_HEADS, HIDDEN, HEAD_DIM), jnp.float32) * sc, 'bv': jnp.zeros((NUM_HEADS, HEAD_DIM), jnp.float32), 'Wo': jax.random.normal(ks[5], (HIDDEN, HIDDEN), jnp.float32) * sc, 'bo': jnp.zeros((HIDDEN,), jnp.float32)}
        return inp
    _L0_xattn_all = _L0_xattn_setup()
    _L0_xattn_in = {k: v for k, v in _L0_xattn_all.items() if k in ('Wq', 'bq', 'Wk', 'bk', 'Wv', 'bv', 'Wo', 'bo')}
    del _L0_xattn_all

    def _L0_ffn_setup():
        import jax, jax.numpy as jnp
        import numpy as np
        B, S, H, I, E_ROUTED, TOP_K = (8, 256, 128, 256, 8, 2)

        def _expert(x, Wg, Wu, Wd):
            return jax.nn.silu(x @ Wg.T) * (x @ Wu.T) @ Wd.T
        key = jax.random.key(seed)
        ks = jax.random.split(key, 9)
        s = 0.02
        return {'x': jax.random.normal(ks[0], (B, S, H), dtype=jnp.float32), 'Wg_s': jax.random.normal(ks[1], (I, H), dtype=jnp.float32) * s, 'Wu_s': jax.random.normal(ks[2], (I, H), dtype=jnp.float32) * s, 'Wd_s': jax.random.normal(ks[3], (H, I), dtype=jnp.float32) * s, 'Wg': jax.random.normal(ks[4], (E_ROUTED, I, H), dtype=jnp.float32) * s, 'Wu': jax.random.normal(ks[5], (E_ROUTED, I, H), dtype=jnp.float32) * s, 'Wd': jax.random.normal(ks[6], (E_ROUTED, H, I), dtype=jnp.float32) * s, 'Wr': jax.random.normal(ks[7], (E_ROUTED, H), dtype=jnp.float32) * s, 'rb': jnp.zeros((E_ROUTED,), dtype=jnp.float32)}
    _L0_ffn_all = _L0_ffn_setup()
    _L0_ffn_in = {k: v for k, v in _L0_ffn_all.items() if k in ('Wg_s', 'Wu_s', 'Wd_s', 'Wg', 'Wu', 'Wd', 'Wr', 'rb')}
    del _L0_ffn_all
    return {'x': x, 'ctx_1024': ctx_1024, 'L0_attn_router_w': _L0_attn_in['router_w'], 'L0_attn_router_b': _L0_attn_in['router_b'], 'L0_attn_wq': _L0_attn_in['wq'], 'L0_attn_wk': _L0_attn_in['wk'], 'L0_attn_wv': _L0_attn_in['wv'], 'L0_xattn_Wq': _L0_xattn_in['Wq'], 'L0_xattn_bq': _L0_xattn_in['bq'], 'L0_xattn_Wk': _L0_xattn_in['Wk'], 'L0_xattn_bk': _L0_xattn_in['bk'], 'L0_xattn_Wv': _L0_xattn_in['Wv'], 'L0_xattn_bv': _L0_xattn_in['bv'], 'L0_xattn_Wo': _L0_xattn_in['Wo'], 'L0_xattn_bo': _L0_xattn_in['bo'], 'L0_ffn_Wg_s': _L0_ffn_in['Wg_s'], 'L0_ffn_Wu_s': _L0_ffn_in['Wu_s'], 'L0_ffn_Wd_s': _L0_ffn_in['Wd_s'], 'L0_ffn_Wg': _L0_ffn_in['Wg'], 'L0_ffn_Wu': _L0_ffn_in['Wu'], 'L0_ffn_Wd': _L0_ffn_in['Wd'], 'L0_ffn_Wr': _L0_ffn_in['Wr'], 'L0_ffn_rb': _L0_ffn_in['rb']}

def reference(x, ctx_1024, L0_attn_router_w, L0_attn_router_b, L0_attn_wq, L0_attn_wk, L0_attn_wv, L0_xattn_Wq, L0_xattn_bq, L0_xattn_Wk, L0_xattn_bk, L0_xattn_Wv, L0_xattn_bv, L0_xattn_Wo, L0_xattn_bo, L0_ffn_Wg_s, L0_ffn_Wu_s, L0_ffn_Wd_s, L0_ffn_Wg, L0_ffn_Wu, L0_ffn_Wd, L0_ffn_Wr, L0_ffn_rb):
    import jax
    import jax.numpy as jnp

    def _L0_attn_ref(x, router_w, router_b, wq, wk, wv):
        import jax, jax.numpy as jnp
        import numpy as np
        import math
        B, L, D = (8, 256, 128)
        HEADS = 1
        HIDDEN = 256
        INNER = HIDDEN // HEADS
        CAPACITY = 0.5
        ROUTER_K = math.ceil(L * CAPACITY)
        b, l, d = x.shape
        inner_dim = wq.shape[0]
        scale = 1.0 / jnp.sqrt(jnp.float32(inner_dim))
        rw = jnp.einsum('bld,d->bl', x, router_w[0]) + router_b[0]
        topk_value, topk_index = jax.lax.top_k(rw, ROUTER_K)
        idx_sorted = jnp.sort(topk_index, axis=1)
        barange = jnp.arange(b)[:, None]
        sel_x = x[barange, idx_sorted]
        s_q = wq[idx_sorted]
        s_k = wk[idx_sorted]
        s_v = wv[idx_sorted]
        q = sel_x * s_q
        k = sel_x * s_k
        v = sel_x * s_v
        score = jnp.einsum('bqd,bkd->bqk', q, k) * scale
        attn = jax.nn.softmax(score, axis=-1)
        s_output = jnp.einsum('bqk,bkd->bqd', attn, v)
        output = jnp.zeros((b, l, d), x.dtype)
        output = output.at[barange, topk_index].set(s_output)
        output = output.at[barange, topk_index].set(x[barange, l - 1 - topk_index])
        return output

    def _L0_xattn_ref(tgt, src, Wq, bq, Wk, bk, Wv, bv, Wo, bo):
        import jax, jax.numpy as jnp
        import numpy as np
        HIDDEN = 128
        NUM_HEADS = 16
        HEAD_DIM = HIDDEN // NUM_HEADS
        q = jnp.einsum('btd,hdk->bhtk', tgt, Wq) + bq[None, :, None, :]
        k = jnp.einsum('bsd,hdk->bhsk', src, Wk) + bk[None, :, None, :]
        v = jnp.einsum('bsd,hdk->bhsk', src, Wv) + bv[None, :, None, :]
        scale = 1.0 / jnp.sqrt(jnp.asarray(HEAD_DIM, q.dtype))
        scores = jnp.einsum('bhtk,bhsk->bhts', q, k) * scale
        weights = jax.nn.softmax(scores, axis=-1)
        out = jnp.einsum('bhts,bhsk->bhtk', weights, v)
        B, H, T, Dh = out.shape
        h = out.transpose(0, 2, 1, 3).reshape(B, T, H * Dh)
        return h @ Wo + bo

    def _L0_ffn_ref(x, Wg_s, Wu_s, Wd_s, Wg, Wu, Wd, Wr, rb):
        import jax, jax.numpy as jnp
        import numpy as np
        B, S, H, I, E_ROUTED, TOP_K = (8, 256, 128, 256, 8, 2)

        def _expert(x, Wg, Wu, Wd):
            return jax.nn.silu(x @ Wg.T) * (x @ Wu.T) @ Wd.T
        shared = _expert(x, Wg_s, Wu_s, Wd_s)
        logits = jnp.einsum('bsh,eh->bse', x, Wr) + rb
        probs = jax.nn.sigmoid(logits)
        scores, idx = jax.lax.top_k(probs, TOP_K)
        cw = (jax.nn.one_hot(idx, E_ROUTED, dtype=x.dtype) * scores[..., None]).sum(-2)
        out = shared
        for e in range(E_ROUTED):
            out = out + cw[..., e:e + 1] * _expert(x, Wg[e], Wu[e], Wd[e])
        return out
    x = _layernorm(x + _L0_attn_ref(x, L0_attn_router_w, L0_attn_router_b, L0_attn_wq, L0_attn_wk, L0_attn_wv), axis=-1)
    x = _layernorm(x + _L0_xattn_ref(x, ctx_1024, L0_xattn_Wq, L0_xattn_bq, L0_xattn_Wk, L0_xattn_bk, L0_xattn_Wv, L0_xattn_bv, L0_xattn_Wo, L0_xattn_bo), axis=-1)
    x = _layernorm(x + _L0_ffn_ref(x, L0_ffn_Wg_s, L0_ffn_Wu_s, L0_ffn_Wd_s, L0_ffn_Wg, L0_ffn_Wu, L0_ffn_Wd, L0_ffn_Wr, L0_ffn_rb), axis=-1)
    return x

_drawn_inputs = setup_inputs


def setup_inputs(seed=0):
    import zlib

    import numpy as np

    out = dict(_drawn_inputs(seed))
    spreads = {'L0_xattn_bq': (0.0, 0.377),
     'L0_xattn_bk': (0.0, 0.8),
     'L0_xattn_bv': (0.0, 0.1),
     'L0_xattn_bo': (0.0, 0.1),
     'L0_ffn_rb': (0.0, 0.8)}
    factors = {'L0_ffn_Wg_s': 6.089,
     'L0_ffn_Wu_s': 5.641,
     'L0_ffn_Wd_s': 5.496,
     'L0_ffn_Wg': 8.0,
     'L0_ffn_Wu': 8.0,
     'L0_ffn_Wd': 8.0,
     'L0_ffn_Wr': 8.0}
    for name, (base, spread) in spreads.items():
        noise = np.random.default_rng([zlib.crc32(name.encode()), seed]).standard_normal(out[name].shape)
        drawn = base * np.exp(spread * noise) if base else spread * noise
        out[name] = jnp.asarray(drawn.astype(out[name].dtype))
    for name, factor in factors.items():
        out[name] = (out[name] * factor).astype(out[name].dtype)
    return out
```

```python
import numpy as np
import concourse.bass as bass
from concourse import mybir
from contextlib import ExitStack

F32 = mybir.dt.float32
BF16 = mybir.dt.bfloat16
ALU = mybir.AluOpType
ACT = mybir.ActivationFunctionType
AX = mybir.AxisListType

P = 128
B, T, S, D = 2, 256, 512, 128
H, DH = 16, 8
INNER, EXPERTS = 256, 8
FFNS = EXPERTS + 1
TT, SC, IC = T // P, S // P, INNER // P
KEEP = T // 2
EPS = 1e-5
SCALE = 1.0 / float(np.sqrt(DH))
BF16_ONES = float(np.array([0x3F803F80], np.uint32).view(np.float32)[0])

Q_PART = [0, 0, 0, 1, 1, 2]
K_PART = [0, 1, 2, 0, 1, 0]
SLOTS, MAX_ROW, PACK = len(Q_PART), 64, 96

GROUPS = 4
UNITS = B * GROUPS * SC
SCORE_TILES = 2
STEPS_PER_GROUP = GROUPS * TT // SCORE_TILES
E_LAG, PV_LAG = 8, 9


def plan():
    extras, experts = {}, {}
    for g in range(B * GROUPS):
        extras.setdefault(4 * g + 5, []).append(("max_rows", g))
    for b in range(B):
        done = GROUPS * SC * (b + 1) + PV_LAG
        for late, kind in ((1, "num_den"), (3, "attn_out"), (6, "x2T"), (7, "logits")):
            extras.setdefault(done + late, []).append((kind, b))
    f = 0
    for n in (33, 36, 39, 42, 43, 44, 45, 46, 47):
        experts[n] = f
        f += 1
    for k in range(FFNS):
        experts[49 + k] = f
        f += 1
    return extras, experts, 49 + FFNS + 1


EXTRAS, EXPERT_AT, STEPS = plan()


def score_tiles(n):
    if n >= B * GROUPS * STEPS_PER_GROUP:
        return []
    g, k = divmod(n, STEPS_PER_GROUP)
    return [(g // GROUPS, g % GROUPS, *divmod(SCORE_TILES * k + x, TT)) for x in range(SCORE_TILES)]


def ring_places():
    order = [("rw_rows",), ("x1T", 0), ("q", 0), ("x1T", 1), ("q", 1)]
    for n in range(STEPS):
        order += [("score", *t) for t in score_tiles(n)] + EXTRAS.get(n, [])
    return {item: k for k, item in enumerate(order)}


def decoder_layer(nc, x_rows, x_flip, router_w, router_b, ctx_t, wq, bq, wk, bk, wv, bv, wo, bo,
                  w_gate, w_up, w_down, w_router, b_router, out):
    ctx = ExitStack()
    with ctx:
        def sb(name, shape, dt=F32):
            return ctx.enter_context(nc.sbuf_tensor(name, shape, dt))

        def sem(name):
            return ctx.enter_context(nc.semaphore(name))

        x_sb = sb("x_sb", [P, B * TT, D])
        flip_sb = sb("flip_sb", [P, B * TT, D])
        rw_w = sb("rw_w", [P, D])
        rw_b = sb("rw_b", [P, 1])
        ctx_sb = sb("ctx_sb", [P, B * S])
        wq_sb, wk_sb, wv_sb, wo_sb = (sb(n, [P, P]) for n in ("wq_sb", "wk_sb", "wv_sb", "wo_sb"))
        bq_sb, bk_sb = sb("bq_sb", [P, 1]), sb("bk_sb", [P, 1])
        bv_sb, bo_sb = sb("bv_sb", [P, H * DH]), sb("bo_sb", [P, D])
        wg_sb = sb("wg_sb", [P, FFNS, INNER])
        wu_sb = sb("wu_sb", [P, FFNS, INNER])
        wd_sb = sb("wd_sb", [P, FFNS, IC, D])
        wr_sb = sb("wr_sb", [P, EXPERTS])
        br_sb = sb("br_sb", [P, EXPERTS])
        ident = sb("ident", [P, P])
        ident_b = sb("ident_b", [P, P], BF16)
        earlier = sb("earlier", [P, TT, T])
        earlier8 = sb("earlier8", [P, TT, EXPERTS, EXPERTS])
        all_one = sb("all_one", [P, T])
        pick = sb("pick", [P, 2, 2, P])
        neg_half = sb("neg_half", [P, TT])
        junk = sb("junk", [P, 2 * B * TT, T])
        rw = sb("rw", [P, B * TT])
        rw_wide = sb("rw_wide", [P, B * TT, P])
        above, ties, rank, kept = (sb(n, [P, B * TT]) for n in ("above", "ties", "rank", "kept"))
        stats = sb("stats", [P, B * TT, 6])
        moments = sb("moments", [P, B * TT, 2])
        var_eps, rstd = sb("var_eps", [P, B * TT]), sb("rstd", [P, B * TT])
        pre_ln = sb("pre_ln", [P, B * TT, D])
        x1 = sb("x1", [P, B * TT, D])
        x1_bo = sb("x1_bo", [P, B * TT, D])
        x1t = sb("x1t", [P, B, T])
        k_part = sb("k_part", [P, B, 3, S], BF16)
        k_rest = sb("k_rest", [P, B, S])
        q_part = sb("q_part", [P, B, 3, T], BF16)
        q_rest = sb("q_rest", [P, B, T])
        k_pack = sb("k_pack", [PACK, B, H, S], BF16)
        q_pack = sb("q_pack", [PACK, B, H, T], BF16)
        v_aug = sb("v_aug", [P, B, SC, H, 32])
        neg_max = sb("neg_max", [P, B * GROUPS, TT, GROUPS])
        max_rest = sb("max_rest", [P, TT, GROUPS])
        max_part = sb("max_part", [P, 2, TT, 3, GROUPS], BF16)
        max_t = sb("max_t", [3 * GROUPS, 2, T], BF16)
        probs = sb("probs", [P, 3, GROUPS, T])
        o_sb = sb("o_sb", [P, 2, T])
        inv_den = sb("inv_den", [P, T])
        ht = sb("ht", [P, T])
        x2 = sb("x2", [P, B * TT, D])
        x2t = sb("x2t", [P, B, T])
        logits = sb("logits", [P, TT, EXPERTS])
        e_neg = sb("e_neg", [P, TT, EXPERTS])
        e_one = sb("e_one", [P, TT, EXPERTS])
        prob = sb("prob", [P, TT, EXPERTS])
        beat = sb("beat", [P, TT, EXPERTS, EXPERTS])
        tie8 = sb("tie8", [P, TT, EXPERTS, EXPERTS])
        rank8 = sb("rank8", [P, TT, EXPERTS])
        top2 = sb("top2", [P, TT, EXPERTS])
        weight = sb("weight", [P, B, TT, EXPERTS])
        tanh = sb("tanh", [P, 2, IC * T])
        gated = sb("gated", [P, 2, IC * T])
        hidden = sb("hidden", [P, 2, IC, T])
        out_sb = sb("out_sb", [P, B * TT, D])

        bank = [ctx.enter_context(nc.psum_tensor(f"bank{i}", [P, 512], F32)) for i in range(8)]
        ring = bank[0:2]
        e_bank = bank[2:4]
        o_bank, g_bank, u_bank, y_bank = bank[4:8]

        ld = {n: sem("ld_" + n) for n in ("x", "flip", "rw", "ctx0", "ctx1", "wk", "wv", "wq", "wo", "bk", "bq",
                                          "bv", "bo", "wg", "wu", "wd", "wr")}
        consts = sem("consts")
        pads = sem("pads")
        v_blank = sem("v_blank")
        q0_pad = sem("q0_pad")
        rw_ready = sem("rw_ready")
        ring_full, ring_free = sem("ring_full"), sem("ring_free")
        k_full, v_full = sem("k_full"), sem("v_full")
        k1_ready, k_rest_ready, k2_ready, k3_ready = (sem(n) for n in ("k1", "k_rest_r", "k2", "k3"))
        q1_ready, q2_ready, q3_ready = (sem(n) for n in ("q1", "q2", "q3"))
        v_ready = sem("v_ready")
        var_ready, rstd_ready = sem("var_ready"), sem("rstd_ready")
        x1_ready, x1_bo_ready = sem("x1_ready"), sem("x1_bo_ready")
        packed = [sem(f"packed{b}") for b in range(B)]
        parts_ready = sem("parts_ready")
        max_in = [sem(f"max_in{g}") for g in range(B * GROUPS)]
        e_full, exp_done, pv_done, o_moved = sem("e_full"), sem("exp_done"), sem("pv_done"), sem("o_moved")
        x2_ready, e_neg_ready = sem("x2_ready"), sem("e_neg_ready")
        g_full, u_full, y_full = sem("g_full"), sem("u_full"), sem("y_full")
        tanh_done, g_free, hidden_ready, y_free = (sem(n) for n in ("tanh_done", "g_free", "hidden_ready", "y_free"))
        out_ready, stored = sem("out_ready"), sem("stored")
        dve_step, pool_step = sem("dve_step"), sem("pool_step")

        place = ring_places()
        block = ctx.enter_context(nc.Block())

        @block.sync
        def _(sp):
            def load(name, dst, src):
                sp.dma_start(dst, src).then_inc(ld[name], 16)

            load("x", x_sb[:, :, :], x_rows)
            load("rw", rw_w[:, :], router_w.to_broadcast([P, D]))
            load("rw", rw_b[:, :], router_b.to_broadcast([P, 1]))
            load("flip", flip_sb[:, :, :], x_flip)
            load("wq", wq_sb[:, :], wq)
            load("bq", bq_sb[:, :], bq)

            def pack_k(b):
                for n, part in sorted(enumerate(K_PART), key=lambda x: x[1]):
                    sp.wait_ge((k1_ready, k2_ready, k3_ready)[part], b + 1)
                    if n == 0:
                        sp.wait_ge(pads, 2 * b + 1)
                    sp.dma_start(k_pack[DH * n:DH * (n + 1), b, :, :], k_part[:, b, part, :]).then_inc(packed[b], 16)

            def pack_q(b):
                for n, part in enumerate(Q_PART):
                    sp.wait_ge((q1_ready, q2_ready, q3_ready)[part], b + 1)
                    if n == 0:
                        sp.wait_ge(q0_pad if b == 0 else pads, 1 if b == 0 else 2)
                    sp.dma_start(q_pack[DH * n:DH * (n + 1), b, :, :], q_part[:, b, part, :]).then_inc(packed[b], 16)

            pack_k(0)
            load("wo", wo_sb[:, :], wo)
            load("bo", bo_sb[:, :], bo.to_broadcast([P, D]))
            pack_q(0)
            load("wr", wr_sb[:, :], w_router)
            load("wr", br_sb[:, :], b_router.to_broadcast([P, EXPERTS]))
            pack_k(1)
            pack_q(1)
            for g in range(B * GROUPS):
                b, i = divmod(g, GROUPS)
                if g == 2:
                    load("wg", wg_sb[:, :, :], w_gate)
                    load("wu", wu_sb[:, :, :], w_up)
                    load("wd", wd_sb[:, :, :, :], w_down)
                sp.wait_ge(ring_free, place[("max_rows", g)] + 1)
                sp.dma_start(q_pack[MAX_ROW:MAX_ROW + 3, b, i:H:GROUPS, :],
                             max_t[:, g % 2, :]).then_inc(max_in[g], 16)
            out_v = out.rearrange("b (t p) d -> p (b t) d", p=P)
            for b in range(B):
                sp.wait_ge(out_ready, b + 1)
                sp.dma_start(out_v[:, TT * b:TT * b + TT, :], out_sb[:, TT * b:TT * b + TT, :]).then_inc(stored, 16)
            sp.wait_ge(stored, 16 * B)

        @block.gpsimd
        def _(pool):
            steps = [0]

            def link(ins):
                steps[0] += 1
                ins.then_inc(pool_step, 1)
                pool.wait_ge(pool_step, steps[0])

            nc.gpsimd.memset(ident[:, :], 0.0)
            nc.gpsimd.memset(earlier[:, :, :], 1.0)
            link(nc.gpsimd.memset(neg_half[:, :], -0.5))
            nc.gpsimd.affine_select(out=ident[:, :], in_=ident[:, :], compare_op=ALU.not_equal, fill=1.0, base=0,
                                    pattern=[[-1, P]], channel_multiplier=1).then_inc(consts, 1)
            nc.gpsimd.affine_select(out=earlier[:, :, :], in_=earlier[:, :, :], compare_op=ALU.is_gt, fill=0.0,
                                    base=0, pattern=[[P, TT], [-1, T]], channel_multiplier=1).then_inc(consts, 1)
            pool.wait_ge(consts, 2)
            nc.gpsimd.memset(k_pack[:, 0, :, :].rearrange("p h s -> p (h s)").bitcast(F32), BF16_ONES).then_inc(pads, 1)

            def power(k, lo, n=TT):
                pool.wait_ge(var_ready, k + 1)
                nc.gpsimd.tensor_tensor(rstd[:, lo:lo + n], var_eps[:, lo:lo + n], neg_half[:, 0:n],
                                        ALU.pow).then_inc(rstd_ready, 1)

            power(0, 0)
            power(1, TT)
            nc.gpsimd.tensor_copy(ident_b[:, :], ident[:, :]).then_inc(consts, 1)
            nc.gpsimd.memset(q_pack[:, 1, :, :].rearrange("p h s -> p (h s)").bitcast(F32), 0.0).then_inc(pads, 1)
            nc.gpsimd.memset(k_pack[:, 1, :, :].rearrange("p h s -> p (h s)").bitcast(F32), BF16_ONES).then_inc(pads, 1)
            link(nc.gpsimd.memset(v_aug[:, :, :, :, :], 0.0))
            v_heads = v_aug[:, :, :, :, :].rearrange("p b c (h a) w -> p (b c h) a w", a=2)
            for a in range(2):
                nc.gpsimd.memset(v_heads[:, :, a, 16 + DH * a:16 + DH * (a + 1)], 1.0).then_inc(v_blank, 1)
            link(nc.gpsimd.memset(pick[:, :, :, :], 0.0))
            for part in range(2):
                for pair in range(2):
                    v = pick[:, part, pair, :].rearrange("p (j c) -> p j c", j=4)[:, :, 16 * pair:16 * pair + 16]
                    nc.gpsimd.affine_select(out=v, in_=v, compare_op=ALU.not_equal, fill=1.0, base=-16 * part,
                                            pattern=[[-32, 4], [-1, 16]], channel_multiplier=1).then_inc(consts, 1)
            link(nc.gpsimd.memset(earlier8[:, :, :, :], 1.0))
            nc.gpsimd.affine_select(out=earlier8[:, :, :, :], in_=earlier8[:, :, :, :], compare_op=ALU.is_gt, fill=0.0,
                                    base=0, pattern=[[0, TT], [1, EXPERTS], [-1, EXPERTS]],
                                    channel_multiplier=0).then_inc(consts, 1)
            pool.wait_ge(ld["bo"], 16)
            for b in range(B):
                pool.wait_ge(x1_ready, b + 1)
                for t in range(TT * b, TT * b + TT):
                    last = nc.gpsimd.tensor_tensor(x1_bo[:, t, :], x1[:, t, :], bo_sb[:, :], ALU.add)
                last.then_inc(x1_bo_ready, 1)
            for k in range(2, 2 + 2 * B):
                b = (0, 1, 0, 1)[k - 2]
                power(k, TT * b)

        @block.scalar
        def _(act):
            def load(name, dst, src):
                act.dma_start(dst, src).then_inc(ld[name], 16)

            load("ctx0", ctx_sb[:, 0:S], ctx_t[:, 0:S])
            load("wk", wk_sb[:, :], wk)
            load("bk", bk_sb[:, :], bk)
            load("ctx1", ctx_sb[:, S:2 * S], ctx_t[:, S:2 * S])
            load("wv", wv_sb[:, :], wv)
            load("bv", bv_sb[:, :], bv.to_broadcast([P, H * DH]))

            def k_parts(b):
                act.wait_ge(k_full, b + 1)
                if b == 0:
                    act.wait_ge(ld["bk"], 16)
                nc.scalar.activation(k_part[:, b, 0, :], (g_bank, u_bank)[b][:, 0:S], ACT.Identity,
                                     bias=bk_sb[:, 0:1]).then_inc(k1_ready, 1)
                act.wait_ge(k_rest_ready, b + 1)
                nc.scalar.copy(k_part[:, b, 1, :], k_rest[:, b, :]).then_inc(k2_ready, 1)

            def q_parts(b):
                act.wait_ge(ring_full, place[("q", b)] + 1)
                if b == 0:
                    act.wait_ge(ld["bq"], 16)
                nc.scalar.activation(q_part[:, b, 0, :], ring[place[("q", b)] % 2][:, 0:T], ACT.Identity,
                                     bias=bq_sb[:, 0:1]).then_inc(q1_ready, 1)
                act.wait_ge(ring_free, place[("q", b)] + 1)
                nc.scalar.copy(q_part[:, b, 1, :], q_rest[:, b, :]).then_inc(q2_ready, 1)

            k_parts(0)
            k_parts(1)
            q_parts(0)
            q_parts(1)

            for n in range(STEPS):
                v = n - PV_LAG - 1
                if 0 <= v < UNITS and v % 8 == 7:
                    act.wait_ge(pv_done, v + 1)
                    nc.scalar.copy(o_sb[:, v // 8 % 2, :], o_bank[:, 0:T]).then_inc(o_moved, 1)
                u = n - E_LAG
                if 0 <= u < UNITS:
                    if u >= 3:
                        act.wait_ge(pv_done, u - 2)
                    for half in range(2):
                        act.wait_ge(e_full, 2 * u + half + 1)
                        nc.scalar.activation(probs[:, u % 3, 2 * half:2 * half + 2, :],
                                             e_bank[half][:, :].rearrange("p (j t) -> p j t", j=2), ACT.Exp,
                                             scale=SCALE).then_inc(exp_done, 1)
                for kind, b in EXTRAS.get(n, []):
                    if kind == "logits":
                        act.wait_ge(ring_free, place[("logits", b)] + 1)
                        nc.scalar.activation(e_neg[:, :, :], logits[:, :, :], ACT.Exp, scale=-1.0).then_inc(e_neg_ready, 1)
                if n in EXPERT_AT:
                    f = EXPERT_AT[n]
                    act.wait_ge(g_full, f + 1)
                    nc.scalar.activation(tanh[:, f % 2, :], g_bank[:, :], ACT.Tanh, scale=0.5).then_inc(tanh_done, 1)

        @block.vector
        def _(dve):
            steps = [0]

            def link(ins):
                steps[0] += 1
                ins.then_inc(dve_step, 1)
                dve.wait_ge(dve_step, steps[0])

            def from_ring(item):
                dve.wait_ge(ring_full, place[item] + 1)
                return ring[place[item] % 2]

            def emptied(item):
                dve.wait_ge(ring_free, place[item] + 1)

            def moments_of(src, lo, k):
                for t in range(lo, lo + TT):
                    last = nc.vector.bn_stats(stats[:, t, :], src[:, t, :])
                link(last)
                for t in range(lo, lo + TT):
                    last = nc.vector.bn_aggr(moments[:, t, :], stats[:, t, :])
                link(last)
                nc.vector.tensor_scalar(var_eps[:, lo:lo + TT], moments[:, lo:lo + TT, 1], EPS, None,
                                        ALU.add).then_inc(var_ready, 1)

            def normalize(dst, src, lo, k, signal, value):
                dve.wait_ge(rstd_ready, k + 1)
                for t in range(lo, lo + TT):
                    last = nc.vector.tensor_scalar(dst[:, t, :], src[:, t, :], moments[:, t, 0:1], rstd[:, t:t + 1],
                                                   ALU.subtract, ALU.mult)
                last.then_inc(signal, 1)

            nc.vector.memset(all_one[:, :], 1.0)
            nc.vector.memset(q_pack[:, 0, :, :].rearrange("p h s -> p (h s)").bitcast(F32), 0.0).then_inc(q0_pad, 1)
            dve.wait_ge(ld["x"], 16)
            dve.wait_ge(ld["rw"], 32)
            for t in range(B * TT):
                last = nc.vector.tensor_tensor_reduce(junk[:, t, 0:D], x_sb[:, t, :], rw_w[:, :], 1.0, 0.0, ALU.mult,
                                                      ALU.add, above[:, t:t + 1])
            link(last)
            link(nc.vector.tensor_scalar(rw[:, :], above[:, :], rw_b[:, 0:1], None, ALU.add))
            for t in range(B * TT):
                last = nc.vector.tensor_scalar(rw_wide[:, t, :], all_one[:, 0:P], rw[:, t:t + 1], None, ALU.mult)
            last.then_inc(rw_ready, 1)

            def k_rest_of(b):
                dve.wait_ge(k1_ready, b + 1)
                nc.vector.scalar_tensor_tensor(out=k_rest[:, b, :], in0=(g_bank, u_bank)[b][:, 0:S], scalar=bk_sb[:, 0:1],
                                               in1=k_part[:, b, 0, :], op0=ALU.add,
                                               op1=ALU.subtract).then_inc(k_rest_ready, 1)

            def k3_of(b):
                dve.wait_ge(k2_ready, b + 1)
                nc.vector.tensor_tensor(k_part[:, b, 2, :], k_rest[:, b, :], k_part[:, b, 1, :],
                                        ALU.subtract).then_inc(k3_ready, 1)

            def q_rest_of(b):
                rows = from_ring(("q", b))
                dve.wait_ge(q1_ready, b + 1)
                nc.vector.scalar_tensor_tensor(out=q_rest[:, b, :], in0=rows[:, 0:T], scalar=bq_sb[:, 0:1],
                                               in1=q_part[:, b, 0, :], op0=ALU.add,
                                               op1=ALU.subtract).then_inc(ring_free, 1)

            def q3_of(b):
                dve.wait_ge(q2_ready, b + 1)
                nc.vector.tensor_tensor(q_part[:, b, 2, :], q_rest[:, b, :], q_part[:, b, 1, :],
                                        ALU.subtract).then_inc(q3_ready, 1)

            def v_of(b):
                dve.wait_ge(v_full, b + 1)
                if b == 0:
                    dve.wait_ge(ld["bv"], 16)
                    dve.wait_ge(v_blank, 2)
                src = (y_bank, o_bank)[b][:, :].rearrange("p (c h a k) -> p c h a k", c=SC, a=2, k=DH)
                dst = v_aug[:, b, :, :, :].rearrange("p c (h a) w -> p c h a w", a=2)
                bias = bv_sb[:, :].rearrange("p (h a k) -> p h a k", a=2, k=DH)
                for a in range(2):
                    for c in range(SC):
                        last = nc.vector.tensor_tensor(dst[:, c, :, a, DH * a:DH * (a + 1)], src[:, c, :, a, :],
                                                       bias[:, :, a, :], ALU.add)
                last.then_inc(v_ready, 1)

            def rank_rows(b):
                lo = TT * b
                if b == 0:
                    dve.wait_ge(consts, 2)
                rows = from_ring(("rw_rows",))[:, T * b:T * b + T]
                for t in range(TT):
                    nc.vector.scalar_tensor_tensor(out=junk[:, 2 * (lo + t), :], in0=rows, scalar=rw[:, lo + t:lo + t + 1],
                                                   in1=all_one[:, :], op0=ALU.is_gt, op1=ALU.mult,
                                                   accum_out=above[:, lo + t:lo + t + 1])
                    last = nc.vector.scalar_tensor_tensor(out=junk[:, 2 * (lo + t) + 1, :], in0=rows, scalar=rw[:, lo + t:lo + t + 1],
                                                          in1=earlier[:, t, :], op0=ALU.is_equal, op1=ALU.mult,
                                                          accum_out=ties[:, lo + t:lo + t + 1])
                if b < B - 1:
                    link(last)
                else:
                    last.then_inc(ring_free, 1)
                    emptied(("rw_rows",))
                link(nc.vector.tensor_tensor(rank[:, lo:lo + TT], above[:, lo:lo + TT], ties[:, lo:lo + TT], ALU.add))
                link(nc.vector.tensor_scalar(kept[:, lo:lo + TT], rank[:, lo:lo + TT], KEEP - 0.5, None, ALU.is_lt))

            def residual_1(b):
                if b == 0:
                    dve.wait_ge(ld["flip"], 16)
                for t in range(TT * b, TT * b + TT):
                    last = nc.vector.scalar_tensor_tensor(out=pre_ln[:, t, :], in0=flip_sb[:, t, :], scalar=kept[:, t:t + 1],
                                                          in1=x_sb[:, t, :], op0=ALU.mult, op1=ALU.add)
                link(last)

            def copy_x1t(b):
                rows = from_ring(("x1T", b))
                nc.vector.tensor_copy(x1t[:, b, :], rows[:, 0:T]).then_inc(ring_free, 1)

            rank_rows(0)
            residual_1(0)
            moments_of(pre_ln, 0, 0)
            k_rest_of(0)
            rank_rows(1)
            normalize(x1, pre_ln, 0, 0, x1_ready, 1)
            k3_of(0)
            residual_1(1)
            moments_of(pre_ln, TT, 1)
            copy_x1t(0)
            k_rest_of(1)
            q_rest_of(0)
            normalize(x1, pre_ln, TT, 1, x1_ready, 2)
            q3_of(0)
            k3_of(1)
            copy_x1t(1)
            q_rest_of(1)
            q3_of(1)
            v_of(0)
            v_of(1)

            def max_parts(g):
                part = max_part[:, g % 2, :, :, :]
                emptied(("score", *divmod(g, GROUPS), GROUPS - 1, TT - 1))
                link(nc.vector.tensor_copy(part[:, :, 0, :], neg_max[:, g, :, :]))
                link(nc.vector.tensor_tensor(max_rest[:, :, :], neg_max[:, g, :, :], part[:, :, 0, :], ALU.subtract))
                link(nc.vector.tensor_copy(part[:, :, 1, :], max_rest[:, :, :]))
                nc.vector.tensor_tensor(part[:, :, 2, :], max_rest[:, :, :], part[:, :, 1, :],
                                        ALU.subtract).then_inc(parts_ready, 1)

            def max_rows(g):
                rows = from_ring(("max_rows", g))
                if g >= 2:
                    dve.wait_ge(max_in[g - 2], 16)
                nc.vector.tensor_copy(max_t[:, g % 2, :], rows[0:3 * GROUPS, 0:T // 2].bitcast(BF16)).then_inc(ring_free, 1)

            def num_den(b):
                rows = from_ring(("num_den", b))
                link(nc.vector.reciprocal(inv_den[:, :], rows[:, T:2 * T]))
                nc.vector.tensor_tensor(ht[:, :], rows[:, 0:T], inv_den[:, :], ALU.mult).then_inc(ring_free, 1)

            def attn_out(b):
                rows = from_ring(("attn_out", b))
                lo = TT * b
                dve.wait_ge(x1_bo_ready, b + 1)
                nc.vector.tensor_tensor(pre_ln[:, lo:lo + TT, :], rows[:, 0:T].rearrange("p (t d) -> p t d", t=TT),
                                        x1_bo[:, lo:lo + TT, :], ALU.add).then_inc(ring_free, 1)
                emptied(("attn_out", b))
                moments_of(pre_ln, lo, 2 + b)
                normalize(x2, pre_ln, lo, 2 + b, x2_ready, b + 1)

            def x2T(b):
                rows = from_ring(("x2T", b))
                nc.vector.tensor_copy(x2t[:, b, :], rows[:, 0:T]).then_inc(ring_free, 1)

            def route(b):
                rows = from_ring(("logits", b))
                shape = [P, TT, EXPERTS, EXPERTS]
                for t in range(TT):
                    last = nc.vector.tensor_tensor(logits[:, t, :], rows[:, EXPERTS * t:EXPERTS * (t + 1)], br_sb[:, :], ALU.add)
                last.then_inc(ring_free, 1)
                dve.wait_ge(e_neg_ready, b + 1)
                link(nc.vector.tensor_scalar(e_one[:, :, :], e_neg[:, :, :], 1.0, None, ALU.add))
                link(nc.vector.reciprocal(prob[:, :, :], e_one[:, :, :]))
                rival = prob[:, :, :].unsqueeze(2).to_broadcast(shape)
                own = prob[:, :, :].unsqueeze(3).to_broadcast(shape)
                nc.vector.tensor_tensor(beat[:, :, :, :], rival, own, ALU.is_gt)
                link(nc.vector.tensor_tensor(tie8[:, :, :, :], rival, own, ALU.is_equal))
                if b == 0:
                    dve.wait_ge(consts, 8)
                link(nc.vector.tensor_tensor(tie8[:, :, :, :], tie8[:, :, :, :], earlier8[:, :, :, :], ALU.mult))
                link(nc.vector.tensor_tensor(beat[:, :, :, :], beat[:, :, :, :], tie8[:, :, :, :], ALU.add))
                link(nc.vector.tensor_reduce(rank8[:, :, :], beat[:, :, :, :], AX.X, ALU.add))
                link(nc.vector.tensor_scalar(top2[:, :, :], rank8[:, :, :], 1.5, 0.5, ALU.is_lt, ALU.mult))
                link(nc.vector.tensor_tensor(weight[:, b, :, :], prob[:, :, :], top2[:, :, :], ALU.mult))

            def combine(f):
                b, e = divmod(f, FFNS)
                dve.wait_ge(y_full, f + 1)
                for t in range(TT):
                    last = nc.vector.scalar_tensor_tensor(
                        out=x2[:, TT * b + t, :], in0=y_bank[:, D * t:D * (t + 1)],
                        scalar=0.5 if e == 0 else weight[:, b, t, e - 1:e], in1=x2[:, TT * b + t, :],
                        op0=ALU.mult, op1=ALU.add)
                last.then_inc(y_free, 1)
                if e == FFNS - 1:
                    dve.wait_ge(y_free, f + 1)
                    moments_of(x2, TT * b, 2 + B + b)
                    normalize(out_sb, x2, TT * b, 2 + B + b, out_ready, b + 1)

            for n in range(STEPS):
                if n and n % STEPS_PER_GROUP == 0 and n // STEPS_PER_GROUP <= B * GROUPS:
                    max_parts(n // STEPS_PER_GROUP - 1)
                for b, i, j, t in score_tiles(n):
                    rows = from_ring(("score", b, i, j, t))
                    nc.vector.tensor_reduce(neg_max[:, GROUPS * b + i, t, j:j + 1], rows[:, :], AX.X, ALU.max,
                                            negate=True).then_inc(ring_free, 1)
                for kind, k in EXTRAS.get(n, []):
                    {"max_rows": max_rows, "num_den": num_den, "attn_out": attn_out, "x2T": x2T, "logits": route}[kind](k)
                if n in EXPERT_AT:
                    f = EXPERT_AT[n]
                    dve.wait_ge(tanh_done, f + 1)
                    nc.vector.scalar_tensor_tensor(out=gated[:, f % 2, :], in0=tanh[:, f % 2, :], scalar=1.0, in1=g_bank[:, :],
                                                   op0=ALU.add, op1=ALU.mult).then_inc(g_free, 1)
                    dve.wait_ge(g_free, f + 1)
                    dve.wait_ge(u_full, f + 1)
                    if f >= 2:
                        dve.wait_ge(y_full, f - 1)
                    nc.vector.tensor_tensor(hidden[:, f % 2, :, :].rearrange("p c t -> p (c t)"), u_bank[:, :], gated[:, f % 2, :],
                                            ALU.mult).then_inc(hidden_ready, 1)
                    if f >= 1:
                        combine(f - 1)
            combine(B * FFNS - 1)

        @block.tensor
        def _(pe):
            def ring_bank(item):
                k = place[item]
                if k >= 2:
                    pe.wait_ge(ring_free, k - 1)
                return ring[k % 2]

            def k_proj(b):
                pe.wait_ge(ld[f"ctx{b}"], 16)
                if b == 0:
                    pe.wait_ge(ld["wk"], 16)
                nc.tensor.matmul((g_bank, u_bank)[b][:, 0:S], wk_sb[:, :], ctx_sb[:, S * b:S * b + S],
                                 start=True, stop=True).then_inc(k_full, 1)

            def v_proj(b):
                if b == 0:
                    pe.wait_ge(ld["wv"], 16)
                for c in range(SC):
                    last = nc.tensor.matmul((y_bank, o_bank)[b][:, P * c:P * c + P], ctx_sb[:, S * b + P * c:S * b + P * c + P],
                                            wv_sb[:, :], start=True, stop=True)
                last.then_inc(v_full, 1)

            def transposed(item, src, ready, value):
                dst = ring_bank(item)
                pe.wait_ge(ready, value)
                for t in range(TT):
                    last = nc.tensor.transpose(dst[:, P * t:P * t + P], src(t), ident[:, :])
                last.then_inc(ring_full, 1)

            def q_proj(b):
                dst = ring_bank(("q", b))
                if b == 0:
                    pe.wait_ge(ld["wq"], 16)
                pe.wait_ge(ring_free, place[("x1T", b)] + 1)
                nc.tensor.matmul(dst[:, 0:T], wq_sb[:, :], x1t[:, b, :], start=True, stop=True).then_inc(ring_full, 1)

            k_proj(0)
            dst = ring_bank(("rw_rows",))
            pe.wait_ge(consts, 1)
            pe.wait_ge(rw_ready, 1)
            for t in range(B * TT):
                last = nc.tensor.transpose(dst[:, P * t:P * t + P], rw_wide[:, t, :], ident[:, :])
            last.then_inc(ring_full, 1)
            k_proj(1)
            v_proj(0)
            v_proj(1)
            for b in range(B):
                transposed(("x1T", b), lambda t: x1[:, TT * b + t, :], x1_ready, b + 1)
                q_proj(b)

            def scores(b, i, j, t):
                dst = ring_bank(("score", b, i, j, t))
                h = GROUPS * j + i
                nc.tensor.matmul(dst[:, :], q_pack[:, b, h, P * t:P * t + P], k_pack[:, b, h, :],
                                 start=True, stop=True).then_inc(ring_full, 1)

            def scores_t(u):
                b, i, c = u // (GROUPS * SC), u // SC % GROUPS, u % SC
                if c == 0:
                    pe.wait_ge(max_in[GROUPS * b + i], 16)
                for half in range(2):
                    if u >= 1:
                        pe.wait_ge(exp_done, 2 * (u - 1) + half + 1)
                    for jj in range(2):
                        h = GROUPS * (2 * half + jj) + i
                        last = nc.tensor.matmul(e_bank[half][:, T * jj:T * jj + T], k_pack[:, b, h, P * c:P * c + P],
                                                q_pack[:, b, h, :], start=True, stop=True)
                    last.then_inc(e_full, 1)

            def p_v(u):
                b, i, c = u // (GROUPS * SC), u // SC % GROUPS, u % SC
                pe.wait_ge(exp_done, 2 * u + 2)
                if u == 0:
                    pe.wait_ge(v_ready, 2)
                if u % 8 == 0 and u:
                    pe.wait_ge(o_moved, u // 8)
                for j in range(4):
                    last = nc.tensor.matmul(o_bank[32 * j:32 * j + 32, 0:T], v_aug[:, b, c, GROUPS * j + i, :],
                                            probs[:, u % 3, j, :], start=(u % 8 == 0), stop=(u % 8 == 7),
                                            tile_position=(0, 32 * j))
                last.then_inc(pv_done, 1)

            def max_rows(g):
                dst = ring_bank(("max_rows", g))
                pe.wait_ge(parts_ready, g + 1)
                if g == 0:
                    pe.wait_ge(consts, 3)
                for t in range(TT):
                    last = nc.tensor.transpose(dst[0:3 * GROUPS, 64 * t:64 * t + 64].bitcast(BF16),
                                               max_part[:, g % 2, t, :, :].rearrange("p a j -> p (a j)"), ident_b[:, :])
                last.then_inc(ring_full, 1)

            def num_den(b):
                dst = ring_bank(("num_den", b))
                if b == 0:
                    pe.wait_ge(consts, 7)
                pe.wait_ge(o_moved, 2 * b + 2)
                for part in range(2):
                    for pair in range(2):
                        last = nc.tensor.matmul(dst[:, T * part:T * part + T], pick[:, part, pair, :], o_sb[:, pair, :],
                                                start=(pair == 0), stop=(pair == 1))
                last.then_inc(ring_full, 1)

            def attn_out(b):
                dst = ring_bank(("attn_out", b))
                if b == 0:
                    pe.wait_ge(ld["wo"], 16)
                pe.wait_ge(ring_free, place[("num_den", b)] + 1)
                for t in range(TT):
                    last = nc.tensor.matmul(dst[:, D * t:D * t + D], ht[:, P * t:P * t + P], wo_sb[:, :], start=True, stop=True)
                last.then_inc(ring_full, 1)

            def x2T(b):
                transposed(("x2T", b), lambda t: x2[:, TT * b + t, :], x2_ready, b + 1)

            def router(b):
                dst = ring_bank(("logits", b))
                if b == 0:
                    pe.wait_ge(ld["wr"], 32)
                pe.wait_ge(ring_free, place[("x2T", b)] + 1)
                for t in range(TT):
                    last = nc.tensor.matmul(dst[:, EXPERTS * t:EXPERTS * (t + 1)], x2t[:, b, P * t:P * t + P], wr_sb[:, :],
                                            start=True, stop=True)
                last.then_inc(ring_full, 1)

            def up(f):
                b, e = divmod(f, FFNS)
                if f == 0:
                    pe.wait_ge(ld["wg"], 16)
                    pe.wait_ge(ld["wu"], 16)
                    pe.wait_ge(k_rest_ready, 2)
                pe.wait_ge(ring_free, place[("x2T", b)] + 1)
                for w, dst, full, used in ((wg_sb, g_bank, g_full, g_free), (wu_sb, u_bank, u_full, hidden_ready)):
                    if f >= 1:
                        pe.wait_ge(used, f)
                    for c in range(IC):
                        last = nc.tensor.matmul(dst[:, T * c:T * c + T], w[:, e, P * c:P * c + P], x2t[:, b, :],
                                                start=True, stop=True)
                    last.then_inc(full, 1)

            def down(f):
                e = f % FFNS
                pe.wait_ge(hidden_ready, f + 1)
                if f == 0:
                    pe.wait_ge(ld["wd"], 16)
                    pe.wait_ge(v_ready, 1)
                else:
                    pe.wait_ge(y_free, f)
                for t in range(TT):
                    for c in range(IC):
                        last = nc.tensor.matmul(y_bank[:, D * t:D * t + D], hidden[:, f % 2, c, P * t:P * t + P],
                                                wd_sb[:, e, c, :], start=(c == 0), stop=(c == IC - 1))
                last.then_inc(y_full, 1)

            for n in range(STEPS):
                if n == 0:
                    pe.wait_ge(packed[0], 16 * 2 * SLOTS)
                if n == GROUPS * STEPS_PER_GROUP:
                    pe.wait_ge(packed[1], 16 * 2 * SLOTS)
                for t in score_tiles(n):
                    scores(*t)
                for kind, k in EXTRAS.get(n, []):
                    {"max_rows": max_rows, "num_den": num_den, "attn_out": attn_out, "x2T": x2T, "logits": router}[kind](k)
                if 0 <= n - E_LAG < UNITS:
                    scores_t(n - E_LAG)
                if 0 <= n - PV_LAG < UNITS:
                    p_v(n - PV_LAG)
                if n in EXPERT_AT:
                    f = EXPERT_AT[n]
                    up(f)
                    if f >= 1:
                        down(f - 1)
            down(B * FFNS - 1)


def kernel(x, ctx_1024, L0_attn_router_w, L0_attn_router_b, L0_attn_wq, L0_attn_wk, L0_attn_wv, L0_xattn_Wq, L0_xattn_bq,
           L0_xattn_Wk, L0_xattn_bk, L0_xattn_Wv, L0_xattn_bv, L0_xattn_Wo, L0_xattn_bo, L0_ffn_Wg_s, L0_ffn_Wu_s,
           L0_ffn_Wd_s, L0_ffn_Wg, L0_ffn_Wu, L0_ffn_Wd, L0_ffn_Wr, L0_ffn_rb):
    import concourse.bacc as bacc
    from concourse.bass_utils import run_bass_kernel_spmd

    a = np.asarray

    def rows(v):
        return a(v).reshape(B * TT, P, D).transpose(1, 0, 2)

    def by_width(w):
        return a(w).transpose(1, 2, 0).reshape(D, DH * H)

    up = [np.concatenate([a(s)[None], a(w)]) for s, w in
          ((L0_ffn_Wg_s, L0_ffn_Wg), (L0_ffn_Wu_s, L0_ffn_Wu), (L0_ffn_Wd_s, L0_ffn_Wd))]
    arrays = {
        "x_rows": rows(x),
        "x_flip": rows(a(x)[:, ::-1]),
        "router_w": a(L0_attn_router_w).reshape(1, D),
        "router_b": a(L0_attn_router_b).reshape(1, 1),
        "ctx_t": a(ctx_1024).reshape(B * S, D).T,
        "wq": by_width(L0_xattn_Wq),
        "bq": a(L0_xattn_bq).T.reshape(P, 1),
        "wk": by_width(L0_xattn_Wk),
        "bk": a(L0_xattn_bk).T.reshape(P, 1),
        "wv": a(L0_xattn_Wv).transpose(1, 0, 2).reshape(D, H * DH),
        "bv": a(L0_xattn_bv).reshape(1, H * DH),
        "wo": a(L0_xattn_Wo),
        "bo": a(L0_xattn_bo).reshape(1, D),
        "w_gate": up[0].transpose(2, 0, 1),
        "w_up": up[1].transpose(2, 0, 1),
        "w_down": up[2].reshape(FFNS, D, IC, P).transpose(3, 0, 2, 1),
        "w_router": a(L0_ffn_Wr).T,
        "b_router": a(L0_ffn_rb).reshape(1, EXPERTS),
    }
    arrays = {f"{n}_dram": np.ascontiguousarray(v) for n, v in arrays.items()}
    nc = bacc.Bacc("TRN2", target_bir_lowering=False, num_devices=1)
    args = [nc.dram_tensor(n, v.shape, mybir.dt.from_np(v.dtype), kind="ExternalInput").ap() for n, v in arrays.items()]
    args.append(nc.dram_tensor("out_dram", (B, T, D), F32, kind="ExternalOutput").ap())
    decoder_layer(nc, *args)
    result = run_bass_kernel_spmd(nc, [arrays], core_ids=[0])
    return result.results[0]["out_dram"]
```

```python
import numpy as np
import concourse.bass as bass
from concourse import mybir
from contextlib import ExitStack

F32 = mybir.dt.float32
BF16 = mybir.dt.bfloat16
F32R = mybir.dt.float32r
ALU = mybir.AluOpType
ACT = mybir.ActivationFunctionType
AX = mybir.AxisListType

P = 128
B, T, S, D = 2, 256, 512, 128
H, DH = 16, 8
INNER, EXPERTS = 256, 8
FFNS = EXPERTS + 1
TT, SC, IC = T // P, S // P, INNER // P
KEEP = T // 2
EPS = 1e-5
SCALE = 1.0 / float(np.sqrt(DH))
BF16_ONES = float(np.array([0x3F803F80], np.uint32).view(np.float32)[0])

Q_PART = [0, 0, 0, 1, 1, 2]
K_PART = [0, 1, 2, 0, 1, 0]
SLOTS, MAX_ROW, PACK = len(Q_PART), 64, 96

GROUPS = 4
UNITS = B * GROUPS * SC
E_LAG, PV_LAG = 8, 9
MAX_LAG = 1


LATE = ((27, 30, 32, 35), (UNITS + PV_LAG, UNITS + PV_LAG + 2, UNITS + PV_LAG + 4, UNITS + PV_LAG + 5))
ROUTE_AT = (39, UNITS + PV_LAG + 8)


def plan():
    extras, experts = {1: [("x1T", 1)], 3: [("q", 1)]}, {}
    for g in range(B * GROUPS):
        extras.setdefault(GROUPS * (g + 1) + MAX_LAG, []).append(("max_rows", g))
    for b in range(B):
        for n, kind in zip(LATE[b], ("num_den", "attn_out", "x2T", "logits")):
            extras.setdefault(n, []).append((kind, b))
    first = UNITS + PV_LAG
    for f in range(B * FFNS):
        experts[first + f] = f
    return extras, experts, first + B * FFNS


EXTRAS, EXPERT_AT, STEPS = plan()


def bank_orders():
    ring, side = [], [("x1T", 0), ("q", 0)]
    for n in range(STEPS):
        ring += [("score", n)] if n < B * H else []
        for item in EXTRAS.get(n, []):
            (ring if item[0] == "num_den" else side).append(item)
    places, user = {}, [0, 0]
    for k, item in enumerate(ring):
        pair = k % 2 if item != ("num_den", 1) else 0
        places[item] = (k, pair, user[pair])
        user[pair] = k + 1
    return places, {item: k for k, item in enumerate(side)}


def decoder_layer(nc, x_rows, x_flip, row_router, ctx_t, wq_bq, wk_bk, wv, wo_wr, bv_bo_br, w_gate, w_up, w_down, out):
    ctx = ExitStack()
    with ctx:
        def sb(name, shape, dt=F32):
            return ctx.enter_context(nc.sbuf_tensor(name, shape, dt))

        def sem(name):
            return ctx.enter_context(nc.semaphore(name))

        x_sb = sb("x_sb", [P, B * TT, D])
        flip_sb = sb("flip_sb", [P, B * TT, D])
        row_sb = sb("row_sb", [P, D + 1])
        rw_w, rw_b = row_sb[:, 0:D], row_sb[:, D:D + 1]
        ctx_sb = sb("ctx_sb", [P, B * S])
        wqb_sb, wkb_sb = sb("wqb_sb", [P, P + 1]), sb("wkb_sb", [P, P + 1])
        wq_sb, bq_sb, wk_sb, bk_sb = wqb_sb[:, 0:P], wqb_sb[:, P:P + 1], wkb_sb[:, 0:P], wkb_sb[:, P:P + 1]
        wv_sb = sb("wv_sb", [P, H * DH])
        wor_sb = sb("wor_sb", [P, D + EXPERTS])
        wo_sb, wr_sb = wor_sb[:, 0:D], wor_sb[:, D:D + EXPERTS]
        bias_sb = sb("bias_sb", [P, 2 * D + EXPERTS])
        bv_sb, bo_sb, br_sb = bias_sb[:, 0:D], bias_sb[:, D:2 * D], bias_sb[:, 2 * D:2 * D + EXPERTS]
        wg_sb = sb("wg_sb", [P, FFNS, INNER])
        wu_sb = sb("wu_sb", [P, FFNS, INNER])
        wd_sb = sb("wd_sb", [P, FFNS, IC, D])
        wg_hi, wg_lo, wu_hi, wu_lo = (sb(n, [P, FFNS, INNER], F32R) for n in ("wg_hi", "wg_lo", "wu_hi", "wu_lo"))
        ident = sb("ident", [P, P])
        ident_b = sb("ident_b", [P, P], BF16)
        earlier = sb("earlier", [P, TT, T])
        earlier8 = sb("earlier8", [P, TT, EXPERTS, EXPERTS])
        all_one = sb("all_one", [P, T])
        pick = sb("pick", [P, 2, 2, P])
        neg_half = sb("neg_half", [P, TT])
        inv_e = sb("inv_e", [P, TT, EXPERTS])
        warm = sb("warm", [P, 1])
        rw = sb("rw", [P, B * TT])
        rw_wide = sb("rw_wide", [P, B * TT, P])
        rw_dot, above, ties, rank, kept = (sb(n, [P, B * TT]) for n in ("rw_dot", "above", "ties", "rank", "kept"))
        stats = sb("stats", [P, B * TT, 6])
        moments = sb("moments", [P, B * TT, 2])
        var_eps, rstd = sb("var_eps", [P, B * TT]), sb("rstd", [P, B * TT])
        pre_ln = sb("pre_ln", [P, B * TT, D])
        x1 = sb("x1", [P, B * TT, D])
        x1_bo = sb("x1_bo", [P, B * TT, D])
        x1t = sb("x1t", [P, B, T])
        k_part = sb("k_part", [P, B, 3, S], BF16)
        k_rest = sb("k_rest", [P, B, S])
        q_part = sb("q_part", [P, B, 3, T], BF16)
        q_rest = sb("q_rest", [P, B, T])
        k_pack = sb("k_pack", [PACK, B, H, S], BF16)
        q_pack = sb("q_pack", [PACK, B, H, T], BF16)
        v_aug = sb("v_aug", [P, B, SC, H, 32])
        neg_max = sb("neg_max", [P, B * GROUPS, TT, GROUPS])
        max_rest = sb("max_rest", [P, TT, GROUPS])
        max_part = sb("max_part", [P, 2, TT, 3, GROUPS], BF16)
        max_t = sb("max_t", [3 * GROUPS, 2, T], BF16)
        probs = sb("probs", [P, 3, GROUPS, T])
        junk = probs[:, :, :, :].rearrange("p s j t -> p (s j) t")
        o_sb = sb("o_sb", [P, 2, T])
        inv_den = sb("inv_den", [P, T])
        ht = sb("ht", [P, T])
        x2 = sb("x2", [P, B * TT, D])
        x2t = sb("x2t", [P, B, T])
        x2t_hi, x2t_lo = sb("x2t_hi", [P, B, T], F32R), sb("x2t_lo", [P, B, T], F32R)
        logits = sb("logits", [P, TT, EXPERTS])
        e_neg = sb("e_neg", [P, TT, EXPERTS])
        e_one = sb("e_one", [P, TT, EXPERTS])
        prob = sb("prob", [P, TT, EXPERTS])
        beat = sb("beat", [P, TT, EXPERTS, EXPERTS])
        tie8 = sb("tie8", [P, TT, EXPERTS, EXPERTS])
        rank8 = sb("rank8", [P, TT, EXPERTS])
        top2 = sb("top2", [P, TT, EXPERTS])
        weight = sb("weight", [P, B, TT, EXPERTS])
        silu = sb("silu", [P, 2, IC * T])
        scaled = sb("scaled", [P, 2, TT * D])
        hidden = sb("hidden", [P, 2, IC, T])
        out_sb = x1

        ring = [ctx.enter_context(nc.psum_tensor(f"ring{i}", [P, 2, 512], F32)) for i in range(2)]
        e_bank = [ctx.enter_context(nc.psum_tensor(f"e_bank{i}", [P, 512], F32)) for i in range(2)]
        o_bank, y_bank = (ctx.enter_context(nc.psum_tensor(n, [P, 512], F32)) for n in ("o_bank", "y_bank"))
        g_bank, u_bank = ring[1][:, 0, :], ring[1][:, 1, :]

        ld = {n: sem("ld_" + n) for n in ("row", "x0", "x1", "flip0", "flip1", "ctx0", "ctx1", "wk", "wv", "wq", "wo",
                                          "bias", "wg", "wu", "wd")}
        consts = sem("consts")
        pads = sem("pads")
        v_blank = sem("v_blank")
        q0_pad = sem("q0_pad")
        rw_ready, rw_rows, ready_to_warm = sem("rw_ready"), sem("rw_rows"), sem("ready_to_warm")
        ring_full, ring_free = sem("ring_full"), sem("ring_free")
        side_full, side_free = sem("side_full"), sem("side_free")
        k_full, v_full = sem("k_full"), sem("v_full")
        k1_ready, k_rest_ready, k2_ready, k3_ready = (sem(n) for n in ("k1", "k_rest_r", "k2", "k3"))
        q1_ready, q2_ready, q3_ready = (sem(n) for n in ("q1", "q2", "q3"))
        v_ready = sem("v_ready")
        var_ready, rstd_ready = sem("var_ready"), sem("rstd_ready")
        x1_ready, x1_bo_ready = sem("x1_ready"), sem("x1_bo_ready")
        packed = [sem(f"packed{b}") for b in range(B)]
        parts_ready = sem("parts_ready")
        max_in = [sem(f"max_in{g}") for g in range(B * GROUPS)]
        e_full, exp_done, pv_done, o_moved = sem("e_full"), sem("exp_done"), sem("pv_done"), sem("o_moved")
        x2_ready, x2t_split, e_neg_ready = sem("x2_ready"), sem("x2t_split"), sem("e_neg_ready")
        w_hi, w_lo = sem("w_hi"), sem("w_lo")
        g_full, u_full, y_full = sem("g_full"), sem("u_full"), sem("y_full")
        silu_done, hidden_ready, y_free = (sem(n) for n in ("silu_done", "hidden_ready", "y_free"))
        scaled_ready, added, weights_ready = sem("scaled_ready"), sem("added"), sem("weights_ready")
        out_ready, stored = sem("out_ready"), sem("stored")
        dve_step, pool_step = sem("dve_step"), sem("pool_step")

        places, side_place = bank_orders()
        place = {item: k for item, (k, _, _) in places.items()}

        def side_bank(item):
            return ring[0][:, 1, :] if item[0] in ("attn_out", "x2T", "logits") and item[1] == 1 else y_bank

        def ring_pair(item):
            return ring[places[item][1]]

        block = ctx.enter_context(nc.Block())

        @block.sync
        def _(sp):
            def load(name, dst, src):
                sp.dma_start(dst, src).then_inc(ld[name], 16)

            load("row", row_sb[:, :], row_router.to_broadcast([P, D + 1]))
            load("x0", x_sb[:, 0:TT, :], x_rows[:, 0:TT, :])
            load("flip0", flip_sb[:, 0:TT, :], x_flip[:, 0:TT, :])
            load("x1", x_sb[:, TT:, :], x_rows[:, TT:, :])
            load("wq", wqb_sb[:, :], wq_bq)
            load("flip1", flip_sb[:, TT:, :], x_flip[:, TT:, :])

            def pack_k(b):
                for n, part in sorted(enumerate(K_PART), key=lambda x: x[1]):
                    sp.wait_ge((k1_ready, k2_ready, k3_ready)[part], b + 1)
                    if n == 0:
                        sp.wait_ge(pads, 2 * b + 1)
                    sp.dma_start(k_pack[DH * n:DH * (n + 1), b, :, :], k_part[:, b, part, :]).then_inc(packed[b], 16)

            def pack_q(b):
                for n, part in enumerate(Q_PART):
                    sp.wait_ge((q1_ready, q2_ready, q3_ready)[part], b + 1)
                    if n == 0:
                        sp.wait_ge(q0_pad if b == 0 else pads, 1 if b == 0 else 2)
                    sp.dma_start(q_pack[DH * n:DH * (n + 1), b, :, :], q_part[:, b, part, :]).then_inc(packed[b], 16)

            pack_k(0)
            pack_q(0)
            load("wg", wg_sb[:, :, :], w_gate)
            load("wu", wu_sb[:, :, :], w_up)
            for g in range(B * GROUPS):
                b, i = divmod(g, GROUPS)
                sp.wait_ge(side_free, side_place[("max_rows", g)] + 1)
                sp.dma_start(q_pack[MAX_ROW:MAX_ROW + 3, b, i:H:GROUPS, :],
                             max_t[:, g % 2, :]).then_inc(max_in[g], 16)
                if g == 0:
                    pack_k(1)
                if g == 1:
                    pack_q(1)
                if g == 2:
                    load("wd", wd_sb[:, :, :, :], w_down)
            out_v = out.rearrange("b (t p) d -> p (b t) d", p=P)
            for b in range(B):
                sp.wait_ge(out_ready, b + 1)
                sp.dma_start(out_v[:, TT * b:TT * b + TT, :], out_sb[:, TT * b:TT * b + TT, :]).then_inc(stored, 16)
            sp.wait_ge(stored, 16 * B)

        @block.gpsimd
        def _(pool):
            steps = [0]

            def link(ins):
                steps[0] += 1
                ins.then_inc(pool_step, 1)
                pool.wait_ge(pool_step, steps[0])

            nc.gpsimd.memset(ident[:, :], 0.0)
            nc.gpsimd.memset(earlier[:, :, :], 1.0)
            link(nc.gpsimd.memset(neg_half[:, :], -0.5))
            nc.gpsimd.affine_select(out=ident[:, :], in_=ident[:, :], compare_op=ALU.not_equal, fill=1.0, base=0,
                                    pattern=[[-1, P]], channel_multiplier=1).then_inc(consts, 1)
            nc.gpsimd.affine_select(out=earlier[:, :, :], in_=earlier[:, :, :], compare_op=ALU.is_gt, fill=0.0,
                                    base=0, pattern=[[P, TT], [-1, T]], channel_multiplier=1).then_inc(consts, 1)
            pool.wait_ge(consts, 2)
            nc.gpsimd.memset(k_pack[:, 0, :, :].rearrange("p h s -> p (h s)").bitcast(F32), BF16_ONES).then_inc(pads, 1)

            def power(k, lo, n=TT):
                pool.wait_ge(var_ready, k + 1)
                nc.gpsimd.tensor_tensor(rstd[:, lo:lo + n], var_eps[:, lo:lo + n], neg_half[:, 0:n],
                                        ALU.pow).then_inc(rstd_ready, 1)

            nc.gpsimd.memset(q_pack[:, 1, :, :].rearrange("p h s -> p (h s)").bitcast(F32), 0.0).then_inc(pads, 1)
            power(0, 0)
            nc.gpsimd.tensor_copy(ident_b[:, :], ident[:, :]).then_inc(consts, 1)
            link(nc.gpsimd.memset(v_aug[:, :, :, :, :], 0.0))
            v_heads = v_aug[:, :, :, :, :].rearrange("p b c (h a) w -> p (b c h) a w", a=2)
            for a in range(2):
                nc.gpsimd.memset(v_heads[:, :, a, 16 + DH * a:16 + DH * (a + 1)], 1.0).then_inc(v_blank, 1)
            power(1, TT)
            nc.gpsimd.memset(k_pack[:, 1, :, :].rearrange("p h s -> p (h s)").bitcast(F32), BF16_ONES).then_inc(pads, 1)
            nc.gpsimd.memset(inv_e[:, :, :], float(np.exp(-1.0)))
            nc.gpsimd.memset(earlier8[:, :, :, :], 1.0)
            link(nc.gpsimd.memset(pick[:, :, :, :], 0.0))
            for part in range(2):
                for pair in range(2):
                    v = pick[:, part, pair, :].rearrange("p (j c) -> p j c", j=4)[:, :, 16 * pair:16 * pair + 16]
                    nc.gpsimd.affine_select(out=v, in_=v, compare_op=ALU.not_equal, fill=1.0, base=-16 * part,
                                            pattern=[[-32, 4], [-1, 16]], channel_multiplier=1).then_inc(consts, 1)
            nc.gpsimd.affine_select(out=earlier8[:, :, :, :], in_=earlier8[:, :, :, :], compare_op=ALU.is_gt, fill=0.0,
                                    base=0, pattern=[[0, TT], [1, EXPERTS], [-1, EXPERTS]],
                                    channel_multiplier=0).then_inc(consts, 1)
            pool.wait_ge(ld["bias"], 16)
            for b in range(B):
                pool.wait_ge(x1_ready, b + 1)
                for t in range(TT * b, TT * b + TT):
                    last = nc.gpsimd.tensor_tensor(x1_bo[:, t, :], x1[:, t, :], bo_sb, ALU.add)
                last.then_inc(x1_bo_ready, 1)
            def split_weights(k):
                pool.wait_ge(w_hi, k + 1)
                w, hi, lo = ((wg_sb, wg_hi, wg_lo), (wu_sb, wu_hi, wu_lo))[k % 2]
                e = slice(3 * (k // 2), 3 * (k // 2) + 3)
                nc.gpsimd.tensor_tensor(lo[:, e, :], w[:, e, :], hi[:, e, :].bitcast(F32), ALU.subtract).then_inc(w_lo, 1)

            def max_parts(g):
                part = max_part[:, g % 2, :, :, :]
                pool.wait_ge(ring_free, place[("score", GROUPS * (g + 1) - 1)] + 1)
                if g >= 2:
                    pool.wait_ge(side_full, side_place[("max_rows", g - 2)] + 1)
                link(nc.gpsimd.tensor_copy(part[:, :, 0, :], neg_max[:, g, :, :]))
                link(nc.gpsimd.tensor_tensor(max_rest[:, :, :], neg_max[:, g, :, :], part[:, :, 0, :], ALU.subtract))
                link(nc.gpsimd.tensor_copy(part[:, :, 1, :], max_rest[:, :, :]))
                nc.gpsimd.tensor_tensor(part[:, :, 2, :], max_rest[:, :, :], part[:, :, 1, :],
                                        ALU.subtract).then_inc(parts_ready, 1)

            def exp_logits(b, t):
                pool.wait_ge(side_free, side_place[("logits", b)] + 1)
                nc.gpsimd.tensor_tensor(e_neg[:, t, :], inv_e[:, t, :], logits[:, t, :], ALU.pow).then_inc(e_neg_ready, 1)

            for g in range(B * GROUPS):
                max_parts(g)
                if g < 3:
                    split_weights(2 * g)
                    split_weights(2 * g + 1)
                if g == 6:
                    power(2, 0)
            for t in range(TT):
                exp_logits(0, t)
            for f in range(B * FFNS):
                b, e = divmod(f, FFNS)
                if f == 2:
                    power(3, TT)
                if e == FFNS - 1:
                    power(2 + B + b, TT * b)
                    continue
                m = f - b
                pool.wait_ge(scaled_ready, m + 1)
                if m:
                    pool.wait_ge(added, m)
                x2_b = x2[:, TT * b:TT * b + TT, :].rearrange("p t d -> p (t d)")
                nc.gpsimd.tensor_tensor(x2_b, x2_b, scaled[:, m % 2, :], ALU.add).then_inc(added, 1)
                if f in (5, 6):
                    exp_logits(1, f - 5)

        @block.scalar
        def _(act):
            def load(name, dst, src):
                act.dma_start(dst, src).then_inc(ld[name], 16)

            load("ctx0", ctx_sb[:, 0:S], ctx_t[:, 0:S])
            load("wk", wkb_sb[:, :], wk_bk)
            load("ctx1", ctx_sb[:, S:2 * S], ctx_t[:, S:2 * S])
            load("wv", wv_sb[:, :], wv)
            load("bias", bias_sb[:, :], bv_bo_br.to_broadcast([P, 2 * D + EXPERTS]))
            load("wo", wor_sb[:, :], wo_wr)
            act.wait_ge(ready_to_warm, 1)
            nc.scalar.activation(warm[:, :], warm[:, :], ACT.Exp)

            def k1_of(b):
                act.wait_ge(k_full, b + 1)
                nc.scalar.activation(k_part[:, b, 0, :], (g_bank, u_bank)[b][:, 0:S], ACT.Identity,
                                     bias=bk_sb).then_inc(k1_ready, 1)

            def k2_of(b):
                act.wait_ge(k_rest_ready, b + 1)
                nc.scalar.copy(k_part[:, b, 1, :], k_rest[:, b, :]).then_inc(k2_ready, 1)

            def q1_of(b):
                act.wait_ge(side_full, side_place[("q", b)] + 1)
                nc.scalar.activation(q_part[:, b, 0, :], side_bank(("q", b))[:, 0:T], ACT.Identity,
                                     bias=bq_sb).then_inc(q1_ready, 1)

            def q2_of(b):
                act.wait_ge(side_free, side_place[("q", b)] + 1)
                nc.scalar.copy(q_part[:, b, 1, :], q_rest[:, b, :]).then_inc(q2_ready, 1)

            k1_of(0)
            k1_of(1)
            k2_of(0)
            q1_of(0)
            q2_of(0)
            k2_of(1)

            def scale_rows(f):
                b, e = divmod(f, FFNS)
                if e == FFNS - 1:
                    return
                act.wait_ge(y_full, f + 1)
                m = f - b
                if m >= 2:
                    act.wait_ge(added, m - 1)
                if e == 0:
                    nc.scalar.copy(scaled[:, m % 2, :], y_bank[:, 0:TT * D]).then_inc(scaled_ready, 1)
                else:
                    if e == 1:
                        act.wait_ge(weights_ready, b + 1)
                    for t in range(TT):
                        last = nc.scalar.activation(scaled[:, m % 2, D * t:D * t + D], y_bank[:, D * t:D * t + D],
                                                    ACT.Copy, scale=weight[:, b, t, e - 1:e])
                    last.then_inc(scaled_ready, 1)

            for n in range(STEPS):
                v = n - PV_LAG - 1
                if 0 <= v < UNITS and v % 8 == 7:
                    act.wait_ge(pv_done, v + 1)
                    nc.scalar.copy(o_sb[:, v // 8 % 2, :], o_bank[:, 0:T]).then_inc(o_moved, 1)
                u = n - E_LAG
                if 0 <= u < UNITS:
                    if u >= 3:
                        act.wait_ge(pv_done, u - 2)
                    for half in range(2):
                        act.wait_ge(e_full, 2 * u + half + 1)
                        nc.scalar.activation(probs[:, u % 3, 2 * half:2 * half + 2, :],
                                             e_bank[half][:, :].rearrange("p (j t) -> p j t", j=2), ACT.Exp,
                                             scale=SCALE).then_inc(exp_done, 1)
                if ("q", 1) in EXTRAS.get(n, []):
                    q1_of(1)
                    q2_of(1)
                for kind, k in EXTRAS.get(n, []):
                    if kind == "max_rows":
                        act.wait_ge(side_full, side_place[("max_rows", k)] + 1)
                        if k >= 2:
                            act.wait_ge(max_in[k - 2], 16)
                        nc.scalar.copy(max_t[:, k % 2, :],
                                       y_bank[0:3 * GROUPS, 0:T // 2].bitcast(BF16)).then_inc(side_free, 1)
                if 4 <= n < 10:
                    k = n - 4
                    w, hi, name = ((wg_sb, wg_hi, "wg"), (wu_sb, wu_hi, "wu"))[k % 2]
                    e = slice(3 * (k // 2), 3 * (k // 2) + 3)
                    if k < 2:
                        act.wait_ge(ld[name], 16)
                    nc.scalar.copy(hi[:, e, :], w[:, e, :]).then_inc(w_hi, 1)
                if n in EXPERT_AT:
                    f = EXPERT_AT[n]
                    act.wait_ge(g_full, f + 1)
                    nc.scalar.activation(silu[:, f % 2, :], g_bank[:, :], ACT.Silu).then_inc(silu_done, 1)
                    if f >= 1:
                        scale_rows(f - 1)

        @block.vector
        def _(dve):
            steps = [0]

            def link(ins):
                steps[0] += 1
                ins.then_inc(dve_step, 1)
                dve.wait_ge(dve_step, steps[0])

            def from_ring(item):
                dve.wait_ge(ring_full, place[item] + 1)
                return ring_pair(item)

            def from_side(item):
                dve.wait_ge(side_full, side_place[item] + 1)
                return side_bank(item)

            def emptied(item):
                dve.wait_ge(side_free, side_place[item] + 1)

            def moments_of(src, lo, k):
                for t in range(lo, lo + TT):
                    last = nc.vector.bn_stats(stats[:, t, :], src[:, t, :])
                link(last)
                for t in range(lo, lo + TT):
                    last = nc.vector.bn_aggr(moments[:, t, :], stats[:, t, :])
                link(last)
                nc.vector.tensor_scalar(var_eps[:, lo:lo + TT], moments[:, lo:lo + TT, 1], EPS, None,
                                        ALU.add).then_inc(var_ready, 1)

            def normalize(dst, src, lo, k, signal, value):
                dve.wait_ge(rstd_ready, k + 1)
                for t in range(lo, lo + TT):
                    last = nc.vector.tensor_scalar(dst[:, t, :], src[:, t, :], moments[:, t, 0:1], rstd[:, t:t + 1],
                                                   ALU.subtract, ALU.mult)
                last.then_inc(signal, 1)

            nc.vector.memset(warm[:, :], 0.0).then_inc(ready_to_warm, 1)
            nc.vector.memset(all_one[:, :], 1.0)
            nc.vector.memset(q_pack[:, 0, :, :].rearrange("p h s -> p (h s)").bitcast(F32), 0.0).then_inc(q0_pad, 1)

            def row_weights(b):
                dve.wait_ge(ld[f"x{b}"], 16)
                lo = TT * b
                if b == 0:
                    dve.wait_ge(ld["row"], 16)
                for t in range(lo, lo + TT):
                    last = nc.vector.tensor_tensor_reduce(junk[:, t, 0:D], x_sb[:, t, :], rw_w, 1.0, 0.0, ALU.mult,
                                                          ALU.add, rw_dot[:, t:t + 1])
                link(last)
                link(nc.vector.tensor_scalar(rw[:, lo:lo + TT], rw_dot[:, lo:lo + TT], rw_b, None, ALU.add))
                for t in range(lo, lo + TT):
                    last = nc.vector.tensor_scalar(rw_wide[:, t, :], all_one[:, 0:P], rw[:, t:t + 1], None, ALU.mult)
                last.then_inc(rw_ready, 1)

            def k_rest_of(b):
                dve.wait_ge(k1_ready, b + 1)
                nc.vector.scalar_tensor_tensor(out=k_rest[:, b, :], in0=(g_bank, u_bank)[b][:, 0:S], scalar=bk_sb,
                                               in1=k_part[:, b, 0, :], op0=ALU.add,
                                               op1=ALU.subtract).then_inc(k_rest_ready, 1)

            def k3_of(b):
                dve.wait_ge(k2_ready, b + 1)
                nc.vector.tensor_tensor(k_part[:, b, 2, :], k_rest[:, b, :], k_part[:, b, 1, :],
                                        ALU.subtract).then_inc(k3_ready, 1)

            def q_rest_of(b):
                rows = from_side(("q", b))
                dve.wait_ge(q1_ready, b + 1)
                nc.vector.scalar_tensor_tensor(out=q_rest[:, b, :], in0=rows[:, 0:T], scalar=bq_sb,
                                               in1=q_part[:, b, 0, :], op0=ALU.add,
                                               op1=ALU.subtract).then_inc(side_free, 1)

            def q3_of(b):
                dve.wait_ge(q2_ready, b + 1)
                nc.vector.tensor_tensor(q_part[:, b, 2, :], q_rest[:, b, :], q_part[:, b, 1, :],
                                        ALU.subtract).then_inc(q3_ready, 1)

            def v_of(b):
                dve.wait_ge(v_full, b + 1)
                if b == 0:
                    dve.wait_ge(ld["bias"], 16)
                    dve.wait_ge(v_blank, 2)
                src = (o_bank, e_bank[1])[b][:, :].rearrange("p (c h a k) -> p c h a k", c=SC, a=2, k=DH)
                dst = v_aug[:, b, :, :, :].rearrange("p c (h a) w -> p c h a w", a=2)
                bias = bv_sb.rearrange("p (h a k) -> p h a k", a=2, k=DH)
                for a in range(2):
                    last = nc.vector.tensor_tensor(dst[:, :, :, a, DH * a:DH * (a + 1)], src[:, :, :, a, :],
                                                   bias[:, :, a, :].unsqueeze(1).to_broadcast([P, SC, H // 2, DH]), ALU.add)
                last.then_inc(v_ready, 1)

            def rank_rows(b):
                lo = TT * b
                if b == 0:
                    dve.wait_ge(consts, 2)
                dve.wait_ge(rw_rows, b + 1)
                rows = e_bank[0][:, T * b:T * b + T]
                for t in range(TT):
                    nc.vector.scalar_tensor_tensor(out=junk[:, 2 * (lo + t), :], in0=rows, scalar=rw[:, lo + t:lo + t + 1],
                                                   in1=all_one[:, :], op0=ALU.is_gt, op1=ALU.mult,
                                                   accum_out=above[:, lo + t:lo + t + 1])
                    last = nc.vector.scalar_tensor_tensor(out=junk[:, 2 * (lo + t) + 1, :], in0=rows, scalar=rw[:, lo + t:lo + t + 1],
                                                          in1=earlier[:, t, :], op0=ALU.is_equal, op1=ALU.mult,
                                                          accum_out=ties[:, lo + t:lo + t + 1])
                link(last)
                link(nc.vector.tensor_tensor(rank[:, lo:lo + TT], above[:, lo:lo + TT], ties[:, lo:lo + TT], ALU.add))
                link(nc.vector.tensor_scalar(kept[:, lo:lo + TT], rank[:, lo:lo + TT], KEEP - 0.5, None, ALU.is_lt))

            def residual_1(b):
                dve.wait_ge(ld[f"flip{b}"], 16)
                for t in range(TT * b, TT * b + TT):
                    last = nc.vector.scalar_tensor_tensor(out=pre_ln[:, t, :], in0=flip_sb[:, t, :], scalar=kept[:, t:t + 1],
                                                          in1=x_sb[:, t, :], op0=ALU.mult, op1=ALU.add)
                link(last)

            def copy_x1t(b):
                rows = from_side(("x1T", b))
                nc.vector.tensor_copy(x1t[:, b, :], rows[:, 0:T]).then_inc(side_free, 1)

            row_weights(0)
            rank_rows(0)
            residual_1(0)
            moments_of(pre_ln, 0, 0)
            k_rest_of(0)
            normalize(x1, pre_ln, 0, 0, x1_ready, 1)
            k3_of(0)
            copy_x1t(0)
            row_weights(1)
            k_rest_of(1)
            q_rest_of(0)
            q3_of(0)
            rank_rows(1)
            residual_1(1)
            moments_of(pre_ln, TT, 1)

            def x1_of_1():
                normalize(x1, pre_ln, TT, 1, x1_ready, 2)

            chores = {0: [x1_of_1], 1: [lambda: k3_of(1)], 2: [lambda: v_of(0)], 4: [lambda: q3_of(1)], 6: [lambda: v_of(1)],
                      ROUTE_AT[0]: [lambda: route(0)], ROUTE_AT[1]: [lambda: route(1)],
                      LATE[0][0]: [lambda: divide(0)], LATE[1][0] + 1: [lambda: divide(1)],
                      LATE[0][1] + 1: [lambda: x2_of(0)], LATE[1][1] + 1: [lambda: x2_of(1)],
                      UNITS + PV_LAG + FFNS + 1: [lambda: out_of(0)]}

            def num_den(b):
                rows = from_ring(("num_den", b))
                nc.vector.reciprocal(inv_den[:, 0:T // 2], rows[:, 1, 0:T // 2])

            def divide(b):
                rows = ring_pair(("num_den", b))
                link(nc.vector.reciprocal(inv_den[:, T // 2:], rows[:, 1, T // 2:T]))
                nc.vector.tensor_tensor(ht[:, :], rows[:, 0, 0:T], inv_den[:, :], ALU.mult).then_inc(ring_free, 1)

            def attn_out(b):
                rows = from_side(("attn_out", b))
                lo = TT * b
                dve.wait_ge(x1_bo_ready, b + 1)
                nc.vector.tensor_tensor(pre_ln[:, lo:lo + TT, :], rows[:, 0:T].rearrange("p (t d) -> p t d", t=TT),
                                        x1_bo[:, lo:lo + TT, :], ALU.add).then_inc(side_free, 1)
                emptied(("attn_out", b))
                moments_of(pre_ln, lo, 2 + b)

            def x2_of(b):
                normalize(x2, pre_ln, TT * b, 2 + b, x2_ready, b + 1)

            def x2T(b):
                rows = from_side(("x2T", b))
                nc.vector.tensor_copy(x2t_hi[:, b, :], rows[:, 0:T])
                nc.vector.tensor_copy(x2t[:, b, :], rows[:, 0:T]).then_inc(side_free, 1)
                emptied(("x2T", b))
                nc.vector.tensor_tensor(x2t_lo[:, b, :], x2t[:, b, :], x2t_hi[:, b, :].bitcast(F32),
                                        ALU.subtract).then_inc(x2t_split, 1)

            def add_router_bias(b):
                rows = from_side(("logits", b))
                for t in range(TT):
                    last = nc.vector.tensor_tensor(logits[:, t, :], rows[:, EXPERTS * t:EXPERTS * (t + 1)], br_sb[:, :], ALU.add)
                last.then_inc(side_free, 1)

            def route(b):
                shape = [P, TT, EXPERTS, EXPERTS]
                dve.wait_ge(e_neg_ready, TT * (b + 1))
                link(nc.vector.tensor_scalar(e_one[:, :, :], e_neg[:, :, :], 1.0, None, ALU.add))
                link(nc.vector.reciprocal(prob[:, :, :], e_one[:, :, :]))
                rival = prob[:, :, :].unsqueeze(2).to_broadcast(shape)
                own = prob[:, :, :].unsqueeze(3).to_broadcast(shape)
                nc.vector.tensor_tensor(beat[:, :, :, :], rival, own, ALU.is_gt)
                link(nc.vector.tensor_tensor(tie8[:, :, :, :], rival, own, ALU.is_equal))
                if b == 0:
                    dve.wait_ge(consts, 8)
                link(nc.vector.tensor_tensor(tie8[:, :, :, :], tie8[:, :, :, :], earlier8[:, :, :, :], ALU.mult))
                link(nc.vector.tensor_tensor(beat[:, :, :, :], beat[:, :, :, :], tie8[:, :, :, :], ALU.add))
                link(nc.vector.tensor_reduce(rank8[:, :, :], beat[:, :, :, :], AX.X, ALU.add))
                link(nc.vector.tensor_scalar(top2[:, :, :], rank8[:, :, :], 1.5, None, ALU.is_lt))
                nc.vector.tensor_tensor(weight[:, b, :, :], prob[:, :, :], top2[:, :, :], ALU.mult).then_inc(weights_ready, 1)

            def finish(b):
                f = FFNS * (b + 1) - 1
                dve.wait_ge(y_full, f + 1)
                dve.wait_ge(added, EXPERTS * (b + 1))
                if b == 0:
                    dve.wait_ge(weights_ready, 1)
                for t in range(TT):
                    last = nc.vector.scalar_tensor_tensor(
                        out=pre_ln[:, TT * b + t, :], in0=y_bank[:, D * t:D * (t + 1)],
                        scalar=weight[:, b, t, EXPERTS - 1:EXPERTS], in1=x2[:, TT * b + t, :], op0=ALU.mult, op1=ALU.add)
                last.then_inc(y_free, 1)
                dve.wait_ge(y_free, b + 1)
                moments_of(pre_ln, TT * b, 2 + B + b)

            def out_of(b):
                normalize(out_sb, pre_ln, TT * b, 2 + B + b, out_ready, b + 1)

            for n in range(STEPS):
                if n < B * H:
                    dve.wait_ge(ring_full, place[("score", n)] + 1)
                    nc.vector.tensor_reduce(neg_max[:, n // GROUPS, :, n % GROUPS], ring_pair(("score", n))[:, :, :], AX.X,
                                            ALU.max, negate=True).then_inc(ring_free, 1)
                if n in EXPERT_AT:
                    f = EXPERT_AT[n]
                    dve.wait_ge(u_full, f + 1)
                    dve.wait_ge(silu_done, f + 1)
                    if f >= 2:
                        dve.wait_ge(y_full, f - 1)
                    nc.vector.tensor_tensor(hidden[:, f % 2, :, :].rearrange("p c t -> p (c t)"), u_bank[:, :], silu[:, f % 2, :],
                                            ALU.mult).then_inc(hidden_ready, 1)
                    if f == FFNS:
                        finish(0)
                for kind, k in EXTRAS.get(n, []):
                    if kind != "max_rows":
                        {"num_den": num_den, "attn_out": attn_out, "x2T": x2T, "logits": add_router_bias,
                         "x1T": copy_x1t, "q": q_rest_of}[kind](k)
                for chore in chores.get(n, []):
                    chore()
            finish(1)
            out_of(1)

        @block.tensor
        def _(pe):
            def ring_bank(item):
                _, pair, free = places[item]
                if free:
                    pe.wait_ge(ring_free, free)
                return ring[pair]

            def k_proj(b):
                pe.wait_ge(ld[f"ctx{b}"], 16)
                if b == 0:
                    pe.wait_ge(ld["wk"], 16)
                nc.tensor.matmul((g_bank, u_bank)[b][:, 0:S], wk_sb, ctx_sb[:, S * b:S * b + S],
                                 start=True, stop=True).then_inc(k_full, 1)

            def v_proj(b):
                if b == 0:
                    pe.wait_ge(ld["wv"], 16)
                for c in range(SC):
                    last = nc.tensor.matmul((o_bank, e_bank[1])[b][:, P * c:P * c + P], ctx_sb[:, S * b + P * c:S * b + P * c + P],
                                            wv_sb[:, :], start=True, stop=True)
                last.then_inc(v_full, 1)

            def to_side(item):
                if side_place[item]:
                    pe.wait_ge(side_free, side_place[item])
                return side_bank(item)

            def transposed(item, src, ready, value):
                dst = to_side(item)
                pe.wait_ge(ready, value)
                for t in range(TT):
                    last = nc.tensor.transpose(dst[:, P * t:P * t + P], src(t), ident[:, :])
                last.then_inc(side_full, 1)

            def q_proj(b):
                dst = to_side(("q", b))
                if b == 0:
                    pe.wait_ge(ld["wq"], 16)
                pe.wait_ge(side_free, side_place[("x1T", b)] + 1)
                nc.tensor.matmul(dst[:, 0:T], wq_sb, x1t[:, b, :], start=True, stop=True).then_inc(side_full, 1)

            def spread_rows(b):
                if b == 0:
                    pe.wait_ge(consts, 1)
                pe.wait_ge(rw_ready, b + 1)
                for t in range(TT):
                    last = nc.tensor.transpose(e_bank[0][:, T * b + P * t:T * b + P * t + P], rw_wide[:, TT * b + t, :], ident[:, :])
                last.then_inc(rw_rows, 1)

            def x1T(b):
                transposed(("x1T", b), lambda t: x1[:, TT * b + t, :], x1_ready, b + 1)

            spread_rows(0)
            k_proj(0)
            k_proj(1)
            v_proj(0)
            v_proj(1)
            x1T(0)
            q_proj(0)
            spread_rows(1)

            def scores(n):
                dst = ring_bank(("score", n))
                if n == 0:
                    pe.wait_ge(k_rest_ready, 2)
                b, i, j = n // H, n // GROUPS % GROUPS, n % GROUPS
                h = GROUPS * j + i
                for t in range(TT):
                    last = nc.tensor.matmul(dst[:, t, :], q_pack[:, b, h, P * t:P * t + P],
                                            k_pack[:, b, h, :], start=True, stop=True)
                last.then_inc(ring_full, 1)

            def scores_t(u):
                b, i, c = u // (GROUPS * SC), u // SC % GROUPS, u % SC
                if u == 0:
                    pe.wait_ge(v_ready, B)
                if c == 0:
                    pe.wait_ge(max_in[GROUPS * b + i], 16)
                for half in range(2):
                    if u >= 1:
                        pe.wait_ge(exp_done, 2 * (u - 1) + half + 1)
                    for jj in range(2):
                        h = GROUPS * (2 * half + jj) + i
                        last = nc.tensor.matmul(e_bank[half][:, T * jj:T * jj + T], k_pack[:, b, h, P * c:P * c + P],
                                                q_pack[:, b, h, :], start=True, stop=True)
                    last.then_inc(e_full, 1)

            def p_v(u):
                b, i, c = u // (GROUPS * SC), u // SC % GROUPS, u % SC
                pe.wait_ge(exp_done, 2 * u + 2)
                if u % 8 == 0 and u:
                    pe.wait_ge(o_moved, u // 8)
                for j in range(4):
                    last = nc.tensor.matmul(o_bank[32 * j:32 * j + 32, 0:T], v_aug[:, b, c, GROUPS * j + i, :],
                                            probs[:, u % 3, j, :], start=(u % 8 == 0), stop=(u % 8 == 7),
                                            tile_position=(0, 32 * j))
                last.then_inc(pv_done, 1)

            def max_rows(g):
                dst = to_side(("max_rows", g))
                pe.wait_ge(parts_ready, g + 1)
                if g == 0:
                    pe.wait_ge(consts, 3)
                for t in range(TT):
                    last = nc.tensor.transpose(dst[0:3 * GROUPS, 64 * t:64 * t + 64].bitcast(BF16),
                                               max_part[:, g % 2, t, :, :].rearrange("p a j -> p (a j)"), ident_b[:, :])
                last.then_inc(side_full, 1)

            def num_den(b):
                dst = ring_bank(("num_den", b))
                if b == 0:
                    pe.wait_ge(consts, 7)
                pe.wait_ge(o_moved, 2 * b + 2)
                for part in range(2):
                    for pair in range(2):
                        last = nc.tensor.matmul(dst[:, part, 0:T], pick[:, part, pair, :], o_sb[:, pair, :],
                                                start=(pair == 0), stop=(pair == 1))
                last.then_inc(ring_full, 1)

            def attn_out(b):
                dst = to_side(("attn_out", b))
                if b == 0:
                    pe.wait_ge(ld["wo"], 16)
                pe.wait_ge(ring_free, place[("num_den", b)] + 1)
                for t in range(TT):
                    last = nc.tensor.matmul(dst[:, D * t:D * t + D], ht[:, P * t:P * t + P], wo_sb, start=True, stop=True)
                last.then_inc(side_full, 1)

            def x2T(b):
                transposed(("x2T", b), lambda t: x2[:, TT * b + t, :], x2_ready, b + 1)

            def router(b):
                dst = to_side(("logits", b))
                pe.wait_ge(side_free, side_place[("x2T", b)] + 1)
                for t in range(TT):
                    last = nc.tensor.matmul(dst[:, EXPERTS * t:EXPERTS * (t + 1)], x2t[:, b, P * t:P * t + P], wr_sb,
                                            start=True, stop=True)
                last.then_inc(side_full, 1)

            def up(f):
                b, e = divmod(f, FFNS)
                if f == 0:
                    pe.wait_ge(w_lo, 6)
                    pe.wait_ge(ring_free, place[("score", B * H - 1)] + 1)
                pe.wait_ge(x2t_split, b + 1)
                for hi, lo, dst, full, used in ((wg_hi, wg_lo, g_bank, g_full, silu_done),
                                                (wu_hi, wu_lo, u_bank, u_full, hidden_ready)):
                    if f >= 1:
                        pe.wait_ge(used, f)
                    for c in range(IC):
                        col = slice(P * c, P * c + P)
                        for k, (w, x) in enumerate(((hi, x2t_hi), (hi, x2t_lo), (lo, x2t_hi))):
                            last = nc.tensor.matmul(dst[:, T * c:T * c + T], w[:, e, col], x[:, b, :],
                                                    start=(k == 0), stop=(k == 2))
                    last.then_inc(full, 1)

            def down(f):
                e = f % FFNS
                pe.wait_ge(hidden_ready, f + 1)
                if f == 0:
                    pe.wait_ge(ld["wd"], 16)
                    pe.wait_ge(side_free, side_place[("attn_out", 1)])
                elif e == 0:
                    pe.wait_ge(y_free, f // FFNS)
                else:
                    pe.wait_ge(scaled_ready, f - f // FFNS)
                for t in range(TT):
                    for c in range(IC):
                        last = nc.tensor.matmul(y_bank[:, D * t:D * t + D], hidden[:, f % 2, c, P * t:P * t + P],
                                                wd_sb[:, e, c, :], start=(c == 0), stop=(c == IC - 1))
                last.then_inc(y_full, 1)

            for n in range(STEPS):
                if n == 0:
                    pe.wait_ge(packed[0], 16 * 2 * SLOTS)
                if n == H:
                    pe.wait_ge(packed[1], 16 * 2 * SLOTS)
                if n < B * H:
                    scores(n)
                if 0 <= n - E_LAG < UNITS:
                    scores_t(n - E_LAG)
                if 0 <= n - PV_LAG < UNITS:
                    p_v(n - PV_LAG)
                if n in EXPERT_AT:
                    up(EXPERT_AT[n])
                for kind, k in EXTRAS.get(n, []):
                    {"max_rows": max_rows, "num_den": num_den, "attn_out": attn_out, "x2T": x2T, "logits": router,
                     "x1T": x1T, "q": q_proj}[kind](k)
                if EXPERT_AT.get(n, 0) >= 1:
                    down(EXPERT_AT[n] - 1)
            down(B * FFNS - 1)


def kernel(x, ctx_1024, L0_attn_router_w, L0_attn_router_b, L0_attn_wq, L0_attn_wk, L0_attn_wv, L0_xattn_Wq, L0_xattn_bq,
           L0_xattn_Wk, L0_xattn_bk, L0_xattn_Wv, L0_xattn_bv, L0_xattn_Wo, L0_xattn_bo, L0_ffn_Wg_s, L0_ffn_Wu_s,
           L0_ffn_Wd_s, L0_ffn_Wg, L0_ffn_Wu, L0_ffn_Wd, L0_ffn_Wr, L0_ffn_rb):
    import concourse.bacc as bacc
    from concourse.bass_utils import run_bass_kernel_spmd

    a = np.asarray

    def rows(v):
        return a(v).reshape(B * TT, P, D).transpose(1, 0, 2)

    def by_width(w):
        return a(w).transpose(1, 2, 0).reshape(D, DH * H)

    up = [np.concatenate([a(s)[None], a(w)]) for s, w in
          ((L0_ffn_Wg_s, L0_ffn_Wg), (L0_ffn_Wu_s, L0_ffn_Wu), (L0_ffn_Wd_s, L0_ffn_Wd))]
    arrays = {
        "x_rows": rows(x),
        "x_flip": rows(a(x)[:, ::-1]),
        "row_router": np.concatenate([a(L0_attn_router_w).reshape(1, D), a(L0_attn_router_b).reshape(1, 1)], 1),
        "ctx_t": a(ctx_1024).reshape(B * S, D).T,
        "wq_bq": np.concatenate([by_width(L0_xattn_Wq), a(L0_xattn_bq).T.reshape(P, 1)], 1),
        "wk_bk": np.concatenate([by_width(L0_xattn_Wk), a(L0_xattn_bk).T.reshape(P, 1)], 1),
        "wv": a(L0_xattn_Wv).transpose(1, 0, 2).reshape(D, H * DH),
        "wo_wr": np.concatenate([a(L0_xattn_Wo), a(L0_ffn_Wr).T], 1),
        "bv_bo_br": np.concatenate([a(L0_xattn_bv).ravel(), a(L0_xattn_bo), a(L0_ffn_rb)])[None],
        "w_gate": up[0].transpose(2, 0, 1),
        "w_up": up[1].transpose(2, 0, 1),
        "w_down": up[2].reshape(FFNS, D, IC, P).transpose(3, 0, 2, 1),
    }
    arrays = {f"{n}_dram": np.ascontiguousarray(v) for n, v in arrays.items()}
    nc = bacc.Bacc("TRN2", target_bir_lowering=False, num_devices=1)
    args = [nc.dram_tensor(n, v.shape, mybir.dt.from_np(v.dtype), kind="ExternalInput").ap() for n, v in arrays.items()]
    args.append(nc.dram_tensor("out_dram", (B, T, D), F32, kind="ExternalOutput").ap())
    decoder_layer(nc, *args)
    result = run_bass_kernel_spmd(nc, [arrays], core_ids=[0])
    return result.results[0]["out_dram"]
```

```python
import numpy as np
import concourse.bass as bass
from concourse import mybir
from contextlib import ExitStack

F32 = mybir.dt.float32
BF16 = mybir.dt.bfloat16
F32R = mybir.dt.float32r
ALU = mybir.AluOpType
ACT = mybir.ActivationFunctionType
AX = mybir.AxisListType

P = 128
B, T, S, D = 2, 256, 512, 128
H, DH = 16, 8
INNER, EXPERTS = 256, 8
FFNS = EXPERTS + 1
TT, SC, IC = T // P, S // P, INNER // P
KEEP = T // 2
EPS = 1e-5
SCALE = 1.0 / float(np.sqrt(DH))
BF16_ONES = float(np.array([0x3F803F80], np.uint32).view(np.float32)[0])

Q_PART = [0, 0, 0, 1, 1, 2]
K_PART = [0, 1, 2, 0, 1, 0]
SLOTS, MAX_ROW, PACK = len(Q_PART), 64, 96

GROUPS = 4
UNITS = B * GROUPS * SC
E_LAG, PV_LAG = 8, 9
FREE_RING = B * H - E_LAG + 1
DOWN_LAG = 2
MAX_LAG = 1
FIRST_EXPERT = UNITS + PV_LAG
LATE = ((31, 34, 37, 39), (FIRST_EXPERT + 1, FIRST_EXPERT + 4, FIRST_EXPERT + 6, FIRST_EXPERT + 8))
ROUTE_AT = (FIRST_EXPERT, FIRST_EXPERT + 11)


def plan():
    extras, experts = {1: [("x1T", 1)], 3: [("q", 1)], 7: [("v", 1)]}, {}
    for g in range(B * GROUPS):
        extras.setdefault(GROUPS * (g + 1) + MAX_LAG, []).append(("max_rows", g))
    for b in range(B):
        for n, kind in zip(LATE[b], ("num_den", "attn_out", "x2T", "logits")):
            extras.setdefault(n, []).append((kind, b))
    for f in range(B * FFNS):
        experts[FIRST_EXPERT + f] = f
    return extras, experts, FIRST_EXPERT + B * FFNS


EXTRAS, EXPERT_AT, STEPS = plan()


def side_order():
    order = [("x1T", 0), ("q", 0)]
    for n in range(STEPS):
        order += EXTRAS.get(n, [])
    return {item: k for k, item in enumerate(order)}


def decoder_layer(nc, x_rows, x_flip, row_router, ctx_t, wq_bq, wk_bk, wv, wo_wr, bv_bo_br, w_gate, w_up, w_down, out):
    ctx = ExitStack()
    with ctx:
        def sb(name, shape, dt=F32):
            return ctx.enter_context(nc.sbuf_tensor(name, shape, dt))

        def sem(name):
            return ctx.enter_context(nc.semaphore(name))

        x_sb = sb("x_sb", [P, B * TT, D])
        flip_sb = sb("flip_sb", [P, B * TT, D])
        row_sb = sb("row_sb", [P, D + 1])
        rw_w, rw_b = row_sb[:, 0:D], row_sb[:, D:D + 1]
        ctx_sb = sb("ctx_sb", [P, B * S])
        wqb_sb, wkb_sb = sb("wqb_sb", [P, P + 1]), sb("wkb_sb", [P, P + 1])
        wq_sb, bq_sb, wk_sb, bk_sb = wqb_sb[:, 0:P], wqb_sb[:, P:P + 1], wkb_sb[:, 0:P], wkb_sb[:, P:P + 1]
        wv_sb = sb("wv_sb", [P, H * DH])
        wor_sb = sb("wor_sb", [P, D + EXPERTS])
        wo_sb, wr_sb = wor_sb[:, 0:D], wor_sb[:, D:D + EXPERTS]
        bias_sb = sb("bias_sb", [P, 2 * D + EXPERTS])
        bv_sb, bo_sb, br_sb = bias_sb[:, 0:D], bias_sb[:, D:2 * D], bias_sb[:, 2 * D:2 * D + EXPERTS]
        wg_sb = sb("wg_sb", [P, FFNS, INNER])
        wu_sb = sb("wu_sb", [P, FFNS, INNER])
        wd_sb = sb("wd_sb", [P, FFNS, IC, D])
        wg_hi, wg_lo, wu_hi, wu_lo = (sb(n, [P, FFNS, INNER], F32R) for n in ("wg_hi", "wg_lo", "wu_hi", "wu_lo"))
        ident = sb("ident", [P, P])
        ident_b = sb("ident_b", [P, P], BF16)
        earlier = sb("earlier", [P, TT, T])
        earlier8 = sb("earlier8", [P, TT, EXPERTS, EXPERTS])
        all_one = sb("all_one", [P, T])
        pick = sb("pick", [P, 2, 2, P], F32R)
        neg_half = sb("neg_half", [P, TT])
        inv_e = sb("inv_e", [P, TT, EXPERTS])
        warm = sb("warm", [P, 1])
        rw = sb("rw", [P, B * TT])
        rw_wide = sb("rw_wide", [P, B * TT, P])
        rw_dot, above, ties, rank, kept = (sb(n, [P, B * TT]) for n in ("rw_dot", "above", "ties", "rank", "kept"))
        stats = sb("stats", [P, B * TT, 6])
        moments = sb("moments", [P, B * TT, 2])
        var_eps, rstd = sb("var_eps", [P, B * TT]), sb("rstd", [P, B * TT])
        pre_ln = sb("pre_ln", [P, B * TT, D])
        x1 = sb("x1", [P, B * TT, D])
        x1_bo = sb("x1_bo", [P, B * TT, D])
        x1t = sb("x1t", [P, B, T])
        k_part = sb("k_part", [P, B, 3, S], BF16)
        k_rest = sb("k_rest", [P, B, S])
        q_part = sb("q_part", [P, B, 3, T], BF16)
        q_rest = sb("q_rest", [P, B, T])
        k_pack = sb("k_pack", [PACK, B, H, S], BF16)
        q_pack = sb("q_pack", [PACK, B, H, T], BF16)
        v_aug = sb("v_aug", [P, B, SC, H, 32])
        neg_max = sb("neg_max", [P, B * GROUPS, TT, GROUPS])
        max_rest = sb("max_rest", [P, TT, GROUPS])
        max_part = sb("max_part", [P, 2, TT, 3, GROUPS], BF16)
        max_t = sb("max_t", [3 * GROUPS, 2, T], BF16)
        probs = sb("probs", [P, 3, GROUPS, T])
        junk = probs[:, :, :, :].rearrange("p s j t -> p (s j) t")
        o_sb = sb("o_sb", [P, 2, T])
        o_hi, o_lo = sb("o_hi", [P, 2, T], F32R), sb("o_lo", [P, 2, T], F32R)
        inv_den = sb("inv_den", [P, T])
        ht = sb("ht", [P, T])
        x2 = sb("x2", [P, B * TT, D])
        x2t = sb("x2t", [P, B, T])
        x2t_hi, x2t_lo = sb("x2t_hi", [P, B, T], F32R), sb("x2t_lo", [P, B, T], F32R)
        logits = sb("logits", [P, TT, EXPERTS])
        e_neg = sb("e_neg", [P, TT, EXPERTS])
        e_one = sb("e_one", [P, TT, EXPERTS])
        prob = sb("prob", [P, TT, EXPERTS])
        beat = sb("beat", [P, TT, EXPERTS, EXPERTS])
        tie8 = sb("tie8", [P, TT, EXPERTS, EXPERTS])
        rank8 = sb("rank8", [P, TT, EXPERTS])
        top2 = sb("top2", [P, TT, EXPERTS])
        weight = sb("weight", [P, B, TT, EXPERTS])
        silu = sb("silu", [P, 2, IC * T])
        scaled = sb("scaled", [P, 2, TT * D])
        pick_32 = scaled[:, :, :].rearrange("p a (b m) -> p a b m", b=2)
        hidden = ctx_sb[:, :].rearrange("p (f c t) -> p f c t", f=2, c=IC)
        out_sb = x1

        ring = [ctx.enter_context(nc.psum_tensor(f"ring{i}", [P, 2, 512], F32)) for i in range(2)]
        e_bank = [ctx.enter_context(nc.psum_tensor(f"e_bank{i}", [P, 512], F32)) for i in range(2)]
        o_bank, y_bank = (ctx.enter_context(nc.psum_tensor(n, [P, 512], F32)) for n in ("o_bank", "y_bank"))
        g_bank, u_bank = (ring[1][:, 0, :], e_bank[0][:, :]), (ring[1][:, 1, :], e_bank[1][:, :])
        down_bank = (y_bank, o_bank)

        ld = {n: sem("ld_" + n) for n in ("row", "x0", "x1", "flip0", "flip1", "ctx0", "ctx1", "wk", "wv", "wq", "wo",
                                          "bias", "wg", "wu", "wd")}
        consts = sem("consts")
        pads = sem("pads")
        v_blank = sem("v_blank")
        q0_pad = sem("q0_pad")
        rw_ready, rw_rows, ready_to_warm = sem("rw_ready"), sem("rw_rows"), sem("ready_to_warm")
        scores_full, maxima = sem("scores_full"), sem("maxima")
        side_full, side_free = sem("side_full"), sem("side_free")
        k_full, v_full = sem("k_full"), sem("v_full")
        k1_ready, k_rest_ready, k2_ready, k3_ready = (sem(n) for n in ("k1", "k_rest_r", "k2", "k3"))
        q1_ready, q2_ready, q3_ready = (sem(n) for n in ("q1", "q2", "q3"))
        v_ready = sem("v_ready")
        var_ready, rstd_ready = sem("var_ready"), sem("rstd_ready")
        x1_ready, x1_bo_ready = sem("x1_ready"), sem("x1_bo_ready")
        packed = [sem(f"packed{b}") for b in range(B)]
        parts_ready, o_split = sem("parts_ready"), sem("o_split")
        max_in = [sem(f"max_in{g}") for g in range(B * GROUPS)]
        e_full, exp_done, pv_done, o_moved = sem("e_full"), sem("exp_done"), sem("pv_done"), sem("o_moved")
        x2_ready, x2t_split, e_neg_ready = sem("x2_ready"), sem("x2t_split"), sem("e_neg_ready")
        w_hi, w_lo = sem("w_hi"), sem("w_lo")
        g_full, u_full, y_full = sem("g_full"), sem("u_full"), sem("y_full")
        silu_done, hidden_ready, y_free = (sem(n) for n in ("silu_done", "hidden_ready", "y_free"))
        scaled_ready, added, weights_ready = sem("scaled_ready"), sem("added"), sem("weights_ready")
        out_ready, stored = sem("out_ready"), sem("stored")
        dve_step, pool_step = sem("dve_step"), sem("pool_step")

        side_place = side_order()

        def exp_bank(u, half):
            return ring[0][:, half, :] if u >= FREE_RING and u % 2 else e_bank[half][:, :]

        def side_bank(item):
            return ring[0][:, 0, :] if item[0] in ("num_den", "attn_out", "x2T", "logits") and item[1] == B - 1 else y_bank

        block = ctx.enter_context(nc.Block())

        @block.sync
        def _(sp):
            def load(name, dst, src):
                sp.dma_start(dst, src).then_inc(ld[name], 16)

            load("x0", x_sb[:, 0:TT, :], x_rows[:, 0:TT, :])
            load("row", row_sb[:, :], row_router.to_broadcast([P, D + 1]))
            load("flip0", flip_sb[:, 0:TT, :], x_flip[:, 0:TT, :])
            load("x1", x_sb[:, TT:, :], x_rows[:, TT:, :])
            load("wq", wqb_sb[:, :], wq_bq)
            load("flip1", flip_sb[:, TT:, :], x_flip[:, TT:, :])

            def pack_k(b):
                for n, part in sorted(enumerate(K_PART), key=lambda x: x[1]):
                    sp.wait_ge((k1_ready, k2_ready, k3_ready)[part], b + 1)
                    if n == 0:
                        sp.wait_ge(pads, 2 * b + 1)
                    sp.dma_start(k_pack[DH * n:DH * (n + 1), b, :, :], k_part[:, b, part, :]).then_inc(packed[b], 16)

            def pack_q(b):
                for n, part in enumerate(Q_PART):
                    sp.wait_ge((q1_ready, q2_ready, q3_ready)[part], b + 1)
                    if n == 0:
                        sp.wait_ge(q0_pad if b == 0 else pads, 1 if b == 0 else 2)
                    sp.dma_start(q_pack[DH * n:DH * (n + 1), b, :, :], q_part[:, b, part, :]).then_inc(packed[b], 16)

            pack_k(0)
            pack_q(0)
            load("wg", wg_sb[:, :, :], w_gate)
            load("wu", wu_sb[:, :, :], w_up)
            for g in range(B * GROUPS):
                b, i = divmod(g, GROUPS)
                sp.wait_ge(side_free, side_place[("max_rows", g)] + 1)
                sp.dma_start(q_pack[MAX_ROW:MAX_ROW + 3, b, i:H:GROUPS, :],
                             max_t[:, g % 2, :]).then_inc(max_in[g], 16)
                if g == 0:
                    pack_k(1)
                if g == 1:
                    pack_q(1)
                if g == 2:
                    load("wd", wd_sb[:, :, :, :], w_down)
            out_v = out.rearrange("b (t p) d -> p (b t) d", p=P)
            for b in range(B):
                sp.wait_ge(out_ready, b + 1)
                sp.dma_start(out_v[:, TT * b:TT * b + TT, :], out_sb[:, TT * b:TT * b + TT, :]).then_inc(stored, 16)
            sp.wait_ge(stored, 16 * B)

        @block.gpsimd
        def _(pool):
            steps = [0]

            def link(ins):
                steps[0] += 1
                ins.then_inc(pool_step, 1)
                pool.wait_ge(pool_step, steps[0])

            nc.gpsimd.memset(ident[:, :], 0.0)
            nc.gpsimd.memset(earlier[:, :, :], 1.0)
            link(nc.gpsimd.memset(neg_half[:, :], -0.5))
            nc.gpsimd.affine_select(out=ident[:, :], in_=ident[:, :], compare_op=ALU.not_equal, fill=1.0, base=0,
                                    pattern=[[-1, P]], channel_multiplier=1).then_inc(consts, 1)
            nc.gpsimd.affine_select(out=earlier[:, :, :], in_=earlier[:, :, :], compare_op=ALU.is_gt, fill=0.0,
                                    base=0, pattern=[[P, TT], [-1, T]], channel_multiplier=1).then_inc(consts, 1)
            pool.wait_ge(consts, 2)
            nc.gpsimd.memset(k_pack[:, 0, :, :].rearrange("p h s -> p (h s)").bitcast(F32), BF16_ONES).then_inc(pads, 1)

            def power(k, lo, n=TT):
                pool.wait_ge(var_ready, k + 1)
                nc.gpsimd.tensor_tensor(rstd[:, lo:lo + n], var_eps[:, lo:lo + n], neg_half[:, 0:n],
                                        ALU.pow).then_inc(rstd_ready, 1)

            nc.gpsimd.memset(q_pack[:, 1, :, :].rearrange("p h s -> p (h s)").bitcast(F32), 0.0).then_inc(pads, 1)
            power(0, 0)
            nc.gpsimd.tensor_copy(ident_b[:, :], ident[:, :]).then_inc(consts, 1)
            link(nc.gpsimd.memset(v_aug[:, :, :, :, :], 0.0))
            v_heads = v_aug[:, :, :, :, :].rearrange("p b c (h a) w -> p (b c h) a w", a=2)
            for a in range(2):
                nc.gpsimd.memset(v_heads[:, :, a, 16 + DH * a:16 + DH * (a + 1)], 1.0).then_inc(v_blank, 1)
            pool.wait_ge(k2_ready, 2)
            nc.gpsimd.tensor_tensor(k_part[:, 1, 2, :], k_rest[:, 1, :], k_part[:, 1, 1, :], ALU.subtract).then_inc(k3_ready, 1)
            power(1, TT)
            nc.gpsimd.memset(k_pack[:, 1, :, :].rearrange("p h s -> p (h s)").bitcast(F32), BF16_ONES).then_inc(pads, 1)
            nc.gpsimd.memset(inv_e[:, :, :], float(np.exp(-1.0)))
            nc.gpsimd.memset(earlier8[:, :, :, :], 1.0)
            link(nc.gpsimd.memset(pick_32[:, :, :, :], 0.0))

            def picks():
                for part in range(2):
                    for pair in range(2):
                        v = pick_32[:, part, pair, :].rearrange("p (j c) -> p j c", j=4)[:, :, 16 * pair:16 * pair + 16]
                        nc.gpsimd.affine_select(out=v, in_=v, compare_op=ALU.not_equal, fill=1.0, base=-16 * part,
                                                pattern=[[-32, 4], [-1, 16]], channel_multiplier=1).then_inc(consts, 1)
                nc.gpsimd.affine_select(out=earlier8[:, :, :, :], in_=earlier8[:, :, :, :], compare_op=ALU.is_gt, fill=0.0,
                                        base=0, pattern=[[0, TT], [1, EXPERTS], [-1, EXPERTS]],
                                        channel_multiplier=0).then_inc(consts, 1)

            def residual_2():
                pool.wait_ge(ld["bias"], 16)
                for b in range(B):
                    pool.wait_ge(x1_ready, b + 1)
                    for t in range(TT * b, TT * b + TT):
                        last = nc.gpsimd.tensor_tensor(x1_bo[:, t, :], x1[:, t, :], bo_sb, ALU.add)
                    last.then_inc(x1_bo_ready, 1)


            def split_weights(k):
                pool.wait_ge(w_hi, k + 1)
                w, hi, lo = ((wg_sb, wg_hi, wg_lo), (wu_sb, wu_hi, wu_lo))[k % 2]
                e = slice(3 * (k // 2), 3 * (k // 2) + 3)
                nc.gpsimd.tensor_tensor(lo[:, e, :], w[:, e, :], hi[:, e, :].bitcast(F32), ALU.subtract).then_inc(w_lo, 1)

            def max_parts(g):
                part = max_part[:, g % 2, :, :, :]
                pool.wait_ge(maxima, GROUPS * (g + 1))
                if g >= 2:
                    pool.wait_ge(side_full, side_place[("max_rows", g - 2)] + 1)
                link(nc.gpsimd.tensor_copy(part[:, :, 0, :], neg_max[:, g, :, :]))
                link(nc.gpsimd.tensor_tensor(max_rest[:, :, :], neg_max[:, g, :, :], part[:, :, 0, :], ALU.subtract))
                link(nc.gpsimd.tensor_copy(part[:, :, 1, :], max_rest[:, :, :]))
                nc.gpsimd.tensor_tensor(part[:, :, 2, :], max_rest[:, :, :], part[:, :, 1, :],
                                        ALU.subtract).then_inc(parts_ready, 1)

            def split_pair(b, pair):
                pool.wait_ge(o_moved, 2 * b + pair + 1)
                if b:
                    pool.wait_ge(side_full, side_place[("num_den", 0)] + 1)
                if b + pair == 0:
                    pool.wait_ge(consts, 7)
                    nc.gpsimd.tensor_copy(pick[:, :, :, :], pick_32[:, :, :, :]).then_inc(consts, 1)
                link(nc.gpsimd.tensor_copy(o_hi[:, pair, :], o_sb[:, pair, :]))
                nc.gpsimd.tensor_tensor(o_lo[:, pair, :], o_sb[:, pair, :], o_hi[:, pair, :].bitcast(F32),
                                        ALU.subtract).then_inc(o_split, 1)

            def exp_logits(b, t):
                pool.wait_ge(side_free, side_place[("logits", b)] + 1)
                nc.gpsimd.tensor_tensor(e_neg[:, t, :], inv_e[:, t, :], logits[:, t, :], ALU.pow).then_inc(e_neg_ready, 1)

            for g in range(B * GROUPS):
                max_parts(g)
                if g == 0:
                    pool.wait_ge(q2_ready, 2)
                    nc.gpsimd.tensor_tensor(q_part[:, 1, 2, :], q_rest[:, 1, :], q_part[:, 1, 1, :], ALU.subtract).then_inc(q3_ready, 1)
                if g in (5, 6):
                    split_pair(0, g - 5)
                if g == 0:
                    picks()
                    residual_2()
                elif g <= 3:
                    split_weights(2 * g - 2)
                    split_weights(2 * g - 1)
            power(2, 0)
            split_pair(1, 0)
            split_pair(1, 1)
            for f in range(B * FFNS):
                b, e = divmod(f, FFNS)
                if f == 2:
                    power(3, TT)
                if e == FFNS - 1:
                    power(2 + B + b, TT * b)
                    continue
                m = f - b
                pool.wait_ge(scaled_ready, m + 1)
                if m:
                    pool.wait_ge(added, m)
                x2_b = x2[:, TT * b:TT * b + TT, :].rearrange("p t d -> p (t d)")
                nc.gpsimd.tensor_tensor(x2_b, x2_b, scaled[:, m % 2, :], ALU.add).then_inc(added, 1)
                if f in (6, 7):
                    exp_logits(1, f - 6)

        @block.scalar
        def _(act):
            def load(name, dst, src):
                act.dma_start(dst, src).then_inc(ld[name], 16)

            load("wk", wkb_sb[:, :], wk_bk)
            load("ctx0", ctx_sb[:, 0:S], ctx_t[:, 0:S])
            load("ctx1", ctx_sb[:, S:2 * S], ctx_t[:, S:2 * S])
            load("wv", wv_sb[:, :], wv)
            load("bias", bias_sb[:, :], bv_bo_br.to_broadcast([P, 2 * D + EXPERTS]))
            load("wo", wor_sb[:, :], wo_wr)
            act.wait_ge(ready_to_warm, 1)
            nc.scalar.activation(warm[:, :], warm[:, :], ACT.Exp)

            def k1_of(b):
                act.wait_ge(k_full, b + 1)
                nc.scalar.activation(k_part[:, b, 0, :], ring[1][:, b, 0:S], ACT.Identity,
                                     bias=bk_sb).then_inc(k1_ready, 1)

            def k2_of(b):
                act.wait_ge(k_rest_ready, b + 1)
                nc.scalar.copy(k_part[:, b, 1, :], k_rest[:, b, :]).then_inc(k2_ready, 1)

            def q1_of(b):
                act.wait_ge(side_full, side_place[("q", b)] + 1)
                nc.scalar.activation(q_part[:, b, 0, :], side_bank(("q", b))[:, 0:T], ACT.Identity,
                                     bias=bq_sb).then_inc(q1_ready, 1)

            def q2_of(b):
                act.wait_ge(side_free, side_place[("q", b)] + 1)
                nc.scalar.copy(q_part[:, b, 1, :], q_rest[:, b, :]).then_inc(q2_ready, 1)

            k1_of(0)
            k1_of(1)
            k2_of(0)
            q1_of(0)
            q2_of(0)
            k2_of(1)

            def scale_rows(f):
                b, e = divmod(f, FFNS)
                if e == FFNS - 1:
                    return
                act.wait_ge(y_full, f + 1)
                m, y = f - b, down_bank[f % 2]
                if m >= 2:
                    act.wait_ge(added, m - 1)
                if e == 0:
                    nc.scalar.copy(scaled[:, m % 2, :], y[:, 0:TT * D]).then_inc(scaled_ready, 1)
                else:
                    if e == 1:
                        act.wait_ge(weights_ready, b + 1)
                    for t in range(TT):
                        last = nc.scalar.activation(scaled[:, m % 2, D * t:D * t + D], y[:, D * t:D * t + D],
                                                    ACT.Copy, scale=weight[:, b, t, e - 1:e])
                    last.then_inc(scaled_ready, 1)

            for n in range(STEPS):
                v = n - PV_LAG - 1
                if 0 <= v < UNITS - 1 and v % 8 == 7:
                    act.wait_ge(pv_done, v + 1)
                    if v // 8 == 2:
                        act.wait_ge(o_split, 1)
                    nc.scalar.copy(o_sb[:, v // 8 % 2, :], o_bank[:, 0:T]).then_inc(o_moved, 1)
                u = n - E_LAG
                if 0 <= u < UNITS:
                    if u >= 3:
                        act.wait_ge(pv_done, u - 2)
                    for half in range(2):
                        act.wait_ge(e_full, 2 * u + half + 1)
                        nc.scalar.activation(probs[:, u % 3, 2 * half:2 * half + 2, :],
                                             exp_bank(u, half).rearrange("p (j t) -> p j t", j=2), ACT.Exp,
                                             scale=SCALE).then_inc(exp_done, 1)
                if ("q", 1) in EXTRAS.get(n, []):
                    q1_of(1)
                if ("q", 1) in EXTRAS.get(n - 1, []):
                    q2_of(1)
                for kind, k in EXTRAS.get(n, []):
                    if kind == "max_rows":
                        act.wait_ge(side_full, side_place[("max_rows", k)] + 1)
                        if k >= 2:
                            act.wait_ge(max_in[k - 2], 16)
                        nc.scalar.copy(max_t[:, k % 2, :],
                                       y_bank[0:3 * GROUPS, 0:T // 2].bitcast(BF16)).then_inc(side_free, 1)
                if 2 <= n < 8:
                    k = n - 2
                    w, hi, name = ((wg_sb, wg_hi, "wg"), (wu_sb, wu_hi, "wu"))[k % 2]
                    e = slice(3 * (k // 2), 3 * (k // 2) + 3)
                    if k < 2:
                        act.wait_ge(ld[name], 16)
                    nc.scalar.copy(hi[:, e, :], w[:, e, :]).then_inc(w_hi, 1)
                if ("logits", 0) in EXTRAS.get(n - 1, []):
                    act.wait_ge(side_free, side_place[("logits", 0)] + 1)
                    nc.scalar.activation(e_neg[:, :, :], logits[:, :, :], ACT.Exp, scale=-1.0).then_inc(e_neg_ready, TT)
                if n in EXPERT_AT:
                    f = EXPERT_AT[n]
                    act.wait_ge(g_full, f + 1)
                    if f >= 2:
                        act.wait_ge(hidden_ready, f - 1)
                    nc.scalar.activation(silu[:, f % 2, :], g_bank[f % 2], ACT.Silu).then_inc(silu_done, 1)
                    if f >= DOWN_LAG:
                        scale_rows(f - DOWN_LAG)

            for f in range(B * FFNS - DOWN_LAG, B * FFNS):
                scale_rows(f)

        @block.vector
        def _(dve):
            steps = [0]

            def link(ins):
                steps[0] += 1
                ins.then_inc(dve_step, 1)
                dve.wait_ge(dve_step, steps[0])

            def from_side(item):
                dve.wait_ge(side_full, side_place[item] + 1)
                return side_bank(item)

            def emptied(item):
                dve.wait_ge(side_free, side_place[item] + 1)

            def moments_of(src, lo, k):
                for t in range(lo, lo + TT):
                    last = nc.vector.bn_stats(stats[:, t, :], src[:, t, :])
                link(last)
                for t in range(lo, lo + TT):
                    last = nc.vector.bn_aggr(moments[:, t, :], stats[:, t, :])
                link(last)
                nc.vector.tensor_scalar(var_eps[:, lo:lo + TT], moments[:, lo:lo + TT, 1], EPS, None,
                                        ALU.add).then_inc(var_ready, 1)

            def normalize(dst, src, lo, k, signal, value):
                dve.wait_ge(rstd_ready, k + 1)
                for t in range(lo, lo + TT):
                    last = nc.vector.tensor_scalar(dst[:, t, :], src[:, t, :], moments[:, t, 0:1], rstd[:, t:t + 1],
                                                   ALU.subtract, ALU.mult)
                last.then_inc(signal, 1)

            nc.vector.memset(warm[:, :], 0.0).then_inc(ready_to_warm, 1)
            nc.vector.memset(all_one[:, :], 1.0)
            nc.vector.memset(q_pack[:, 0, :, :].rearrange("p h s -> p (h s)").bitcast(F32), 0.0).then_inc(q0_pad, 1)

            def row_weights(b):
                dve.wait_ge(ld[f"x{b}"], 16)
                lo = TT * b
                if b == 0:
                    dve.wait_ge(ld["row"], 16)
                for t in range(lo, lo + TT):
                    last = nc.vector.tensor_tensor_reduce(junk[:, t, 0:D], x_sb[:, t, :], rw_w, 1.0, 0.0, ALU.mult,
                                                          ALU.add, rw_dot[:, t:t + 1])
                link(last)
                link(nc.vector.tensor_scalar(rw[:, lo:lo + TT], rw_dot[:, lo:lo + TT], rw_b, None, ALU.add))
                for t in range(lo, lo + TT):
                    last = nc.vector.tensor_scalar(rw_wide[:, t, :], all_one[:, 0:P], rw[:, t:t + 1], None, ALU.mult)
                last.then_inc(rw_ready, 1)

            def k_rest_of(b):
                dve.wait_ge(k1_ready, b + 1)
                nc.vector.scalar_tensor_tensor(out=k_rest[:, b, :], in0=ring[1][:, b, 0:S], scalar=bk_sb,
                                               in1=k_part[:, b, 0, :], op0=ALU.add,
                                               op1=ALU.subtract).then_inc(k_rest_ready, 1)

            def k3_of(b):
                dve.wait_ge(k2_ready, b + 1)
                nc.vector.tensor_tensor(k_part[:, b, 2, :], k_rest[:, b, :], k_part[:, b, 1, :],
                                        ALU.subtract).then_inc(k3_ready, 1)

            def q_rest_of(b):
                rows = from_side(("q", b))
                dve.wait_ge(q1_ready, b + 1)
                nc.vector.scalar_tensor_tensor(out=q_rest[:, b, :], in0=rows[:, 0:T], scalar=bq_sb,
                                               in1=q_part[:, b, 0, :], op0=ALU.add,
                                               op1=ALU.subtract).then_inc(side_free, 1)

            def q3_of(b):
                dve.wait_ge(q2_ready, b + 1)
                nc.vector.tensor_tensor(q_part[:, b, 2, :], q_rest[:, b, :], q_part[:, b, 1, :],
                                        ALU.subtract).then_inc(q3_ready, 1)

            def v_of(b):
                src = o_bank if b == 0 else from_side(("v", 1))
                if b == 0:
                    dve.wait_ge(v_full, 1)
                    dve.wait_ge(ld["bias"], 16)
                    dve.wait_ge(v_blank, 2)
                src = src[:, :].rearrange("p (c h a k) -> p c h a k", c=SC, a=2, k=DH)
                dst = v_aug[:, b, :, :, :].rearrange("p c (h a) w -> p c h a w", a=2)
                bias = bv_sb.rearrange("p (h a k) -> p h a k", a=2, k=DH)
                for a in range(2):
                    last = nc.vector.tensor_tensor(dst[:, :, :, a, DH * a:DH * (a + 1)], src[:, :, :, a, :],
                                                   bias[:, :, a, :].unsqueeze(1).to_broadcast([P, SC, H // 2, DH]), ALU.add)
                last.then_inc(v_ready if b == 0 else side_free, 1)

            def rank_rows(b):
                lo = TT * b
                if b == 0:
                    dve.wait_ge(consts, 2)
                dve.wait_ge(rw_rows, b + 1)
                rows = e_bank[0][:, T * b:T * b + T]
                for t in range(TT):
                    nc.vector.scalar_tensor_tensor(out=junk[:, 2 * (lo + t), :], in0=rows, scalar=rw[:, lo + t:lo + t + 1],
                                                   in1=all_one[:, :], op0=ALU.is_gt, op1=ALU.mult,
                                                   accum_out=above[:, lo + t:lo + t + 1])
                    last = nc.vector.scalar_tensor_tensor(out=junk[:, 2 * (lo + t) + 1, :], in0=rows, scalar=rw[:, lo + t:lo + t + 1],
                                                          in1=earlier[:, t, :], op0=ALU.is_equal, op1=ALU.mult,
                                                          accum_out=ties[:, lo + t:lo + t + 1])
                link(last)
                link(nc.vector.tensor_tensor(rank[:, lo:lo + TT], above[:, lo:lo + TT], ties[:, lo:lo + TT], ALU.add))
                link(nc.vector.tensor_scalar(kept[:, lo:lo + TT], rank[:, lo:lo + TT], KEEP - 0.5, None, ALU.is_lt))

            def residual_1(b):
                dve.wait_ge(ld[f"flip{b}"], 16)
                for t in range(TT * b, TT * b + TT):
                    last = nc.vector.scalar_tensor_tensor(out=pre_ln[:, t, :], in0=flip_sb[:, t, :], scalar=kept[:, t:t + 1],
                                                          in1=x_sb[:, t, :], op0=ALU.mult, op1=ALU.add)
                link(last)

            def copy_x1t(b):
                rows = from_side(("x1T", b))
                nc.vector.tensor_copy(x1t[:, b, :], rows[:, 0:T]).then_inc(side_free, 1)

            row_weights(0)
            rank_rows(0)
            residual_1(0)
            moments_of(pre_ln, 0, 0)
            k_rest_of(0)
            normalize(x1, pre_ln, 0, 0, x1_ready, 1)
            k3_of(0)
            copy_x1t(0)
            row_weights(1)
            k_rest_of(1)
            q_rest_of(0)
            q3_of(0)
            rank_rows(1)
            residual_1(1)
            moments_of(pre_ln, TT, 1)

            def last_pair():
                dve.wait_ge(pv_done, UNITS)
                dve.wait_ge(o_split, 2)
                nc.vector.tensor_copy(o_sb[:, 1, :], o_bank[:, 0:T]).then_inc(o_moved, 1)

            def num_den(b):
                rows = from_side(("num_den", b))
                nc.vector.reciprocal(inv_den[:, 0:T // 2], rows[:, T:T + T // 2])

            def divide(b):
                rows = side_bank(("num_den", b))
                link(nc.vector.reciprocal(inv_den[:, T // 2:], rows[:, T + T // 2:2 * T]))
                nc.vector.tensor_tensor(ht[:, :], rows[:, 0:T], inv_den[:, :], ALU.mult).then_inc(side_free, 1)

            def attn_out(b):
                rows = from_side(("attn_out", b))
                lo = TT * b
                dve.wait_ge(x1_bo_ready, b + 1)
                nc.vector.tensor_tensor(pre_ln[:, lo:lo + TT, :], rows[:, 0:T].rearrange("p (t d) -> p t d", t=TT),
                                        x1_bo[:, lo:lo + TT, :], ALU.add).then_inc(side_free, 1)
                emptied(("attn_out", b))
                moments_of(pre_ln, lo, 2 + b)

            def x2_of(b):
                normalize(x2, pre_ln, TT * b, 2 + b, x2_ready, b + 1)

            def x2T(b):
                rows = from_side(("x2T", b))
                nc.vector.tensor_copy(x2t_hi[:, b, :], rows[:, 0:T])
                nc.vector.tensor_copy(x2t[:, b, :], rows[:, 0:T]).then_inc(side_free, 1)
                emptied(("x2T", b))
                nc.vector.tensor_tensor(x2t_lo[:, b, :], x2t[:, b, :], x2t_hi[:, b, :].bitcast(F32),
                                        ALU.subtract).then_inc(x2t_split, 1)

            def add_router_bias(b):
                rows = from_side(("logits", b))
                for t in range(TT):
                    last = nc.vector.tensor_tensor(logits[:, t, :], rows[:, EXPERTS * t:EXPERTS * (t + 1)], br_sb[:, :], ALU.add)
                last.then_inc(side_free, 1)

            def route(b):
                shape = [P, TT, EXPERTS, EXPERTS]
                dve.wait_ge(e_neg_ready, TT * (b + 1))
                link(nc.vector.tensor_scalar(e_one[:, :, :], e_neg[:, :, :], 1.0, None, ALU.add))
                link(nc.vector.reciprocal(prob[:, :, :], e_one[:, :, :]))
                rival = prob[:, :, :].unsqueeze(2).to_broadcast(shape)
                own = prob[:, :, :].unsqueeze(3).to_broadcast(shape)
                nc.vector.tensor_tensor(beat[:, :, :, :], rival, own, ALU.is_gt)
                link(nc.vector.tensor_tensor(tie8[:, :, :, :], rival, own, ALU.is_equal))
                if b == 0:
                    dve.wait_ge(consts, 8)
                link(nc.vector.tensor_tensor(tie8[:, :, :, :], tie8[:, :, :, :], earlier8[:, :, :, :], ALU.mult))
                link(nc.vector.tensor_tensor(beat[:, :, :, :], beat[:, :, :, :], tie8[:, :, :, :], ALU.add))
                link(nc.vector.tensor_reduce(rank8[:, :, :], beat[:, :, :, :], AX.X, ALU.add))
                link(nc.vector.tensor_scalar(top2[:, :, :], rank8[:, :, :], 1.5, None, ALU.is_lt))
                nc.vector.tensor_tensor(weight[:, b, :, :], prob[:, :, :], top2[:, :, :], ALU.mult).then_inc(weights_ready, 1)

            def finish(b):
                f = FFNS * (b + 1) - 1
                dve.wait_ge(y_full, f + 1)
                dve.wait_ge(added, EXPERTS * (b + 1))
                if b == 0:
                    dve.wait_ge(weights_ready, 1)
                for t in range(TT):
                    last = nc.vector.scalar_tensor_tensor(
                        out=pre_ln[:, TT * b + t, :], in0=down_bank[f % 2][:, D * t:D * (t + 1)],
                        scalar=weight[:, b, t, EXPERTS - 1:EXPERTS], in1=x2[:, TT * b + t, :], op0=ALU.mult, op1=ALU.add)
                last.then_inc(y_free, 1)
                dve.wait_ge(y_free, b + 1)
                moments_of(pre_ln, TT * b, 2 + B + b)

            def out_of(b):
                normalize(out_sb, pre_ln, TT * b, 2 + B + b, out_ready, b + 1)

            v_of(0)
            normalize(x1, pre_ln, TT, 1, x1_ready, 2)

            for n in range(STEPS):
                if n < B * H:
                    dve.wait_ge(scores_full, n + 1)
                    nc.vector.tensor_reduce(neg_max[:, n // GROUPS, :, n % GROUPS], ring[n % 2][:, :, :], AX.X,
                                            ALU.max, negate=True).then_inc(maxima, 1)
                if n in EXPERT_AT:
                    f = EXPERT_AT[n]
                    dve.wait_ge(u_full, f + 1)
                    dve.wait_ge(silu_done, f + 1)
                    if f >= 2:
                        dve.wait_ge(y_full, f - 1)
                    nc.vector.tensor_tensor(hidden[:, f % 2, :, :].rearrange("p c t -> p (c t)"), u_bank[f % 2], silu[:, f % 2, :],
                                            ALU.mult).then_inc(hidden_ready, 1)
                    if f == FFNS - 1 + DOWN_LAG:
                        finish(0)
                if ("q", 1) in EXTRAS.get(n - 1, []):
                    q_rest_of(1)
                if n == FIRST_EXPERT - 1:
                    last_pair()
                for kind, k in EXTRAS.get(n, []):
                    if kind not in ("max_rows", "q"):
                        {"num_den": num_den, "attn_out": attn_out, "x2T": x2T, "logits": add_router_bias,
                         "x1T": copy_x1t, "v": v_of}[kind](k)
                for b in range(B):
                    num_den_at, attn_out_at = LATE[b][0:2]
                    if n == num_den_at + 1:
                        divide(b)
                    if n == attn_out_at + 1:
                        x2_of(b)
                    if n == ROUTE_AT[b]:
                        route(b)
                if n == FIRST_EXPERT + FFNS + DOWN_LAG + 1:
                    out_of(0)
            finish(1)
            out_of(1)

        @block.tensor
        def _(pe):
            def k_proj(b):
                pe.wait_ge(ld[f"ctx{b}"], 16)
                if b == 0:
                    pe.wait_ge(ld["wk"], 16)
                nc.tensor.matmul(ring[1][:, b, 0:S], wk_sb, ctx_sb[:, S * b:S * b + S],
                                 start=True, stop=True).then_inc(k_full, 1)

            def v_proj(b):
                dst = o_bank if b == 0 else to_side(("v", 1))
                if b == 0:
                    pe.wait_ge(ld["wv"], 16)
                for c in range(SC):
                    last = nc.tensor.matmul(dst[:, P * c:P * c + P], ctx_sb[:, S * b + P * c:S * b + P * c + P],
                                            wv_sb[:, :], start=True, stop=True)
                last.then_inc(v_full if b == 0 else side_full, 1)

            def to_side(item):
                if side_place[item]:
                    pe.wait_ge(side_free, side_place[item])
                return side_bank(item)

            def transposed(item, src, ready, value):
                dst = to_side(item)
                pe.wait_ge(ready, value)
                for t in range(TT):
                    last = nc.tensor.transpose(dst[:, P * t:P * t + P], src(t), ident[:, :])
                last.then_inc(side_full, 1)

            def q_proj(b):
                dst = to_side(("q", b))
                if b == 0:
                    pe.wait_ge(ld["wq"], 16)
                pe.wait_ge(side_free, side_place[("x1T", b)] + 1)
                nc.tensor.matmul(dst[:, 0:T], wq_sb, x1t[:, b, :], start=True, stop=True).then_inc(side_full, 1)

            def spread_rows(b):
                if b == 0:
                    pe.wait_ge(consts, 1)
                pe.wait_ge(rw_ready, b + 1)
                for t in range(TT):
                    last = nc.tensor.transpose(e_bank[0][:, T * b + P * t:T * b + P * t + P], rw_wide[:, TT * b + t, :], ident[:, :])
                last.then_inc(rw_rows, 1)

            def x1T(b):
                transposed(("x1T", b), lambda t: x1[:, TT * b + t, :], x1_ready, b + 1)

            spread_rows(0)
            k_proj(0)
            k_proj(1)
            v_proj(0)
            x1T(0)
            q_proj(0)
            spread_rows(1)

            def scores(n):
                dst = ring[n % 2]
                if n >= 2:
                    pe.wait_ge(maxima, n - 1)
                if n == 1:
                    pe.wait_ge(k_rest_ready, 2)
                b, i, j = n // H, n // GROUPS % GROUPS, n % GROUPS
                h = GROUPS * j + i
                for t in range(TT):
                    last = nc.tensor.matmul(dst[:, t, :], q_pack[:, b, h, P * t:P * t + P],
                                            k_pack[:, b, h, :], start=True, stop=True)
                last.then_inc(scores_full, 1)

            def scores_t(u):
                b, i, c = u // (GROUPS * SC), u // SC % GROUPS, u % SC
                if u == 0:
                    pe.wait_ge(var_ready, B)
                if c == 0:
                    pe.wait_ge(max_in[GROUPS * b + i], 16)
                if u == FREE_RING:
                    pe.wait_ge(maxima, B * H)
                for half in range(2):
                    if u != FREE_RING and u >= 1:
                        pe.wait_ge(exp_done, 2 * (u - (1 if u < FREE_RING else 2)) + half + 1)
                    for jj in range(2):
                        h = GROUPS * (2 * half + jj) + i
                        last = nc.tensor.matmul(exp_bank(u, half)[:, T * jj:T * jj + T], k_pack[:, b, h, P * c:P * c + P],
                                                q_pack[:, b, h, :], start=True, stop=True)
                    last.then_inc(e_full, 1)

            def p_v(u):
                b, i, c = u // (GROUPS * SC), u // SC % GROUPS, u % SC
                pe.wait_ge(exp_done, 2 * u + 2)
                if u == 0:
                    pe.wait_ge(v_ready, 1)
                if u == GROUPS * SC:
                    pe.wait_ge(side_free, side_place[("v", 1)] + 1)
                if u % 8 == 0 and u:
                    pe.wait_ge(o_moved, u // 8)
                for j in range(4):
                    last = nc.tensor.matmul(o_bank[32 * j:32 * j + 32, 0:T], v_aug[:, b, c, GROUPS * j + i, :],
                                            probs[:, u % 3, j, :], start=(u % 8 == 0), stop=(u % 8 == 7),
                                            tile_position=(0, 32 * j))
                last.then_inc(pv_done, 1)

            def max_rows(g):
                dst = to_side(("max_rows", g))
                pe.wait_ge(parts_ready, g + 1)
                if g == 0:
                    pe.wait_ge(consts, 3)
                for t in range(TT):
                    last = nc.tensor.transpose(dst[0:3 * GROUPS, 64 * t:64 * t + 64].bitcast(BF16),
                                               max_part[:, g % 2, t, :, :].rearrange("p a j -> p (a j)"), ident_b[:, :])
                last.then_inc(side_full, 1)

            def num_den(b):
                dst = to_side(("num_den", b))
                if b == 0:
                    pe.wait_ge(consts, 9)
                pe.wait_ge(o_split, 2 * b + 2)
                for part in range(2):
                    for pair in range(2):
                        for k, o in enumerate((o_hi, o_lo)):
                            last = nc.tensor.matmul(dst[:, T * part:T * part + T], pick[:, part, pair, :], o[:, pair, :],
                                                    start=(pair + k == 0), stop=(pair + k == 2))
                last.then_inc(side_full, 1)

            def attn_out(b):
                dst = to_side(("attn_out", b))
                if b == 0:
                    pe.wait_ge(ld["wo"], 16)
                pe.wait_ge(side_free, side_place[("num_den", b)] + 1)
                for t in range(TT):
                    last = nc.tensor.matmul(dst[:, D * t:D * t + D], ht[:, P * t:P * t + P], wo_sb, start=True, stop=True)
                last.then_inc(side_full, 1)

            def x2T(b):
                transposed(("x2T", b), lambda t: x2[:, TT * b + t, :], x2_ready, b + 1)

            def router(b):
                dst = to_side(("logits", b))
                pe.wait_ge(side_free, side_place[("x2T", b)] + 1)
                for t in range(TT):
                    last = nc.tensor.matmul(dst[:, EXPERTS * t:EXPERTS * (t + 1)], x2t[:, b, P * t:P * t + P], wr_sb,
                                            start=True, stop=True)
                last.then_inc(side_full, 1)

            def up(f):
                b, e = divmod(f, FFNS)
                if f == 0:
                    pe.wait_ge(w_lo, 6)
                    pe.wait_ge(maxima, B * H)
                if f == 1:
                    pe.wait_ge(exp_done, 2 * UNITS)
                pe.wait_ge(x2t_split, b + 1)
                for hi, lo, dst, full, used in ((wg_hi, wg_lo, g_bank, g_full, silu_done),
                                                (wu_hi, wu_lo, u_bank, u_full, hidden_ready)):
                    if f >= 2:
                        pe.wait_ge(used, f - 1)
                    for c in range(IC):
                        col = slice(P * c, P * c + P)
                        for k, (w, x) in enumerate(((hi, x2t_hi), (hi, x2t_lo), (lo, x2t_hi))):
                            last = nc.tensor.matmul(dst[f % 2][:, T * c:T * c + T], w[:, e, col], x[:, b, :],
                                                    start=(k == 0), stop=(k == 2))
                    last.then_inc(full, 1)

            def down(f):
                e = f % FFNS
                pe.wait_ge(hidden_ready, f + 1)
                if f == 0:
                    pe.wait_ge(ld["wd"], 16)
                    pe.wait_ge(side_free, side_place[("num_den", 1)])
                elif f == 1:
                    pe.wait_ge(o_moved, 2 * B)
                elif (f - 2) % FFNS == FFNS - 1:
                    pe.wait_ge(y_free, (f - 2) // FFNS + 1)
                else:
                    pe.wait_ge(scaled_ready, f - 2 - (f - 2) // FFNS + 1)
                for t in range(TT):
                    for c in range(IC):
                        last = nc.tensor.matmul(down_bank[f % 2][:, D * t:D * t + D], hidden[:, f % 2, c, P * t:P * t + P],
                                                wd_sb[:, e, c, :], start=(c == 0), stop=(c == IC - 1))
                last.then_inc(y_full, 1)

            for n in range(STEPS):
                if n == 0:
                    pe.wait_ge(packed[0], 16 * 2 * SLOTS)
                if n == H:
                    pe.wait_ge(packed[1], 16 * 2 * SLOTS)
                if n < B * H:
                    scores(n)
                if 0 <= n - E_LAG < UNITS:
                    scores_t(n - E_LAG)
                if 0 <= n - PV_LAG < UNITS:
                    p_v(n - PV_LAG)
                if n in EXPERT_AT:
                    up(EXPERT_AT[n])
                for kind, k in EXTRAS.get(n, []):
                    {"max_rows": max_rows, "num_den": num_den, "attn_out": attn_out, "x2T": x2T, "logits": router,
                     "x1T": x1T, "q": q_proj, "v": v_proj}[kind](k)
                if EXPERT_AT.get(n, 0) >= DOWN_LAG:
                    down(EXPERT_AT[n] - DOWN_LAG)
            for f in range(B * FFNS - DOWN_LAG, B * FFNS):
                down(f)


def kernel(x, ctx_1024, L0_attn_router_w, L0_attn_router_b, L0_attn_wq, L0_attn_wk, L0_attn_wv, L0_xattn_Wq, L0_xattn_bq,
           L0_xattn_Wk, L0_xattn_bk, L0_xattn_Wv, L0_xattn_bv, L0_xattn_Wo, L0_xattn_bo, L0_ffn_Wg_s, L0_ffn_Wu_s,
           L0_ffn_Wd_s, L0_ffn_Wg, L0_ffn_Wu, L0_ffn_Wd, L0_ffn_Wr, L0_ffn_rb):
    import concourse.bacc as bacc
    from concourse.bass_utils import run_bass_kernel_spmd

    a = np.asarray

    def rows(v):
        return a(v).reshape(B * TT, P, D).transpose(1, 0, 2)

    def by_width(w):
        return a(w).transpose(1, 2, 0).reshape(D, DH * H)

    up = [np.concatenate([a(s)[None], a(w)]) for s, w in
          ((L0_ffn_Wg_s, L0_ffn_Wg), (L0_ffn_Wu_s, L0_ffn_Wu), (L0_ffn_Wd_s, L0_ffn_Wd))]
    arrays = {
        "x_rows": rows(x),
        "x_flip": rows(a(x)[:, ::-1]),
        "row_router": np.concatenate([a(L0_attn_router_w).reshape(1, D), a(L0_attn_router_b).reshape(1, 1)], 1),
        "ctx_t": a(ctx_1024).reshape(B * S, D).T,
        "wq_bq": np.concatenate([by_width(L0_xattn_Wq), a(L0_xattn_bq).T.reshape(P, 1)], 1),
        "wk_bk": np.concatenate([by_width(L0_xattn_Wk), a(L0_xattn_bk).T.reshape(P, 1)], 1),
        "wv": a(L0_xattn_Wv).transpose(1, 0, 2).reshape(D, H * DH),
        "wo_wr": np.concatenate([a(L0_xattn_Wo), a(L0_ffn_Wr).T], 1),
        "bv_bo_br": np.concatenate([a(L0_xattn_bv).ravel(), a(L0_xattn_bo), a(L0_ffn_rb)])[None],
        "w_gate": up[0].transpose(2, 0, 1),
        "w_up": up[1].transpose(2, 0, 1),
        "w_down": up[2].reshape(FFNS, D, IC, P).transpose(3, 0, 2, 1),
    }
    arrays = {f"{n}_dram": np.ascontiguousarray(v) for n, v in arrays.items()}
    nc = bacc.Bacc("TRN2", target_bir_lowering=False, num_devices=1)
    args = [nc.dram_tensor(n, v.shape, mybir.dt.from_np(v.dtype), kind="ExternalInput").ap() for n, v in arrays.items()]
    args.append(nc.dram_tensor("out_dram", (B, T, D), F32, kind="ExternalOutput").ap())
    decoder_layer(nc, *args)
    result = run_bass_kernel_spmd(nc, [arrays], core_ids=[0])
    return result.results[0]["out_dram"]
```
